# Optimizing a Trainium2 kernel written in Bass

```python
import numpy as np
import jax
import jax.numpy as jnp

def _softmax(x, axis=-1):
    return jax.nn.softmax(x, axis=axis)

def _gelu(x):
    return jax.nn.gelu(x, approximate=True)

def _silu(x):
    return jax.nn.silu(x)

def _sigmoid(x):
    return jax.nn.sigmoid(x)

def _layernorm(x, axis=-1, eps=1e-05):
    m = jnp.mean(x, axis=axis, keepdims=True)
    v = jnp.var(x, axis=axis, keepdims=True)
    return (x - m) / jnp.sqrt(v + eps)

def _scatter_add(tgt, idx, src, axis=0):
    return tgt.at[idx].add(src)

def _segment_sum(src, seg, n):
    return jax.ops.segment_sum(src, seg, n)
kernel_name = 'mk_macaron_d1_jaxref_r4_e4f333'

def setup_inputs(seed: int=0):
    np.random.seed(seed)
    _w = jnp.asarray

    def _L0_attn_setup():
        import jax, jax.numpy as jnp
        import numpy as np
        from jax import lax
        B, L, D = (2, 1024, 512)
        K, KQ, M, H = (32, 4, 8, 8)
        MEM = K * H
        FLAT = K * H * M
        CONV_W = 4
        DIM_SWIGLU = H * 3 * 2
        N_DECAY = K - 4

        def _forward(x, W_mem, conv_k, W_q, theta, decay_slopes, anchor_slopes, score_scale, W_re, W_im, norm_scale, W_out):
            b, l, d = x.shape
            z = x @ W_mem
            z = lax.conv_general_dilated(z, conv_k, window_strides=(1,), padding=[(CONV_W - 1, 0)], dimension_numbers=('NHC', 'HIO', 'NHC'), feature_group_count=MEM + K)
            k_val = z[..., :MEM].reshape(b, l, K, H)
            s_raw = z[..., MEM:].reshape(b, l, K, 1)
            q = (x @ W_q).reshape(b, l, KQ, H, M, 2)
            q_re, q_im = (q[..., 0], q[..., 1])
            pos = jnp.arange(l, dtype=jnp.float32)
            slopes_d = jax.nn.softplus(decay_slopes).reshape(1, 1, -1, 1)
            slopes_a = jax.nn.softplus(anchor_slopes).reshape(1, 1, -1, 1)
            dist = jnp.maximum(jnp.float32(l - 1) - pos, 0.0)
            log_w = jnp.concatenate([-slopes_d * dist[None, :, None, None], -slopes_a * pos[None, :, None, None]], axis=2)
            log_p = jnp.clip(score_scale[None, None, :, None] * s_raw, -20.0, 20.0)
            p_w = jnp.exp(log_p + log_w)
            phi = k_val[..., None] * theta
            re_k, im_k = (jnp.cos(phi), jnp.sin(phi))
            pw5 = p_w[..., None]
            merged = jnp.concatenate([p_w.squeeze(-1), (pw5 * re_k).reshape(b, l, FLAT), (pw5 * im_k).reshape(b, l, FLAT)], axis=-1)
            cs = jnp.cumsum(merged, axis=1)
            den = cs[..., :K]
            num_re = cs[..., K:K + FLAT]
            num_im = cs[..., K + FLAT:]
            inv_den = 1.0 / jnp.maximum(den[..., None], 0.0001)
            state_re = num_re.reshape(b, l, K, H, M) * inv_den[..., None]
            state_im = num_im.reshape(b, l, K, H, M) * inv_den[..., None]
            n_rep = K // KQ
            q_re = jnp.repeat(q_re, n_rep, axis=2)
            q_im = jnp.repeat(q_im, n_rep, axis=2)
            out_re = jnp.sum(state_re * q_re + state_im * q_im, axis=-1)
            out_im = jnp.sum(state_im * q_re - state_re * q_im, axis=-1)
            out_re = out_re * norm_scale
            out_im = out_im * norm_scale
            y = jnp.einsum('blkh,khn->blkn', out_re, W_re) + jnp.einsum('blkh,khn->blkn', out_im, W_im)
            y_val, y_gate = jnp.split(y, 2, axis=-1)
            y = (y_val * jax.nn.silu(y_gate)).reshape(b, l, -1)
            return y @ W_out
        key = jax.random.key(seed)
        ks = jax.random.split(key, 8)
        x = jax.random.normal(ks[0], (B, L, D), dtype=jnp.float32)
        W_mem = jax.random.normal(ks[1], (D, MEM + K), dtype=jnp.float32) / np.sqrt(D)
        conv_k = jax.random.normal(ks[2], (CONV_W, 1, MEM + K), dtype=jnp.float32) * 0.3
        W_q = jax.random.normal(ks[3], (D, KQ * H * M * 2), dtype=jnp.float32) / np.sqrt(D)
        theta = jnp.asarray(np.tile(np.geomspace(0.001, 3.0, M).reshape(1, 1, 1, 1, M), (1, 1, K, H, 1)), dtype=jnp.float32)
        decay_slopes = jnp.asarray(np.log(np.expm1(np.geomspace(0.001, 0.1, N_DECAY))), dtype=jnp.float32)
        anchor_slopes = jnp.asarray(np.log(np.expm1(np.geomspace(0.01, 0.1, 4))), dtype=jnp.float32)
        score_scale = jnp.ones((K,), dtype=jnp.float32)
        g = np.sqrt(2.0 / (H + DIM_SWIGLU))
        W_re = jax.random.normal(ks[4], (K, H, DIM_SWIGLU), dtype=jnp.float32) * g
        W_im = jax.random.normal(ks[5], (K, H, DIM_SWIGLU), dtype=jnp.float32) * g
        norm_scale = jnp.ones((1, 1, K, H), dtype=jnp.float32)
        W_out = jax.random.normal(ks[6], (K * H * 3, D), dtype=jnp.float32) / np.sqrt(K * H * 3)
        return {'x': x, 'W_mem': W_mem, 'conv_k': conv_k, 'W_q': W_q, 'theta': theta, 'decay_slopes': decay_slopes, 'anchor_slopes': anchor_slopes, 'score_scale': score_scale, 'W_re': W_re, 'W_im': W_im, 'norm_scale': norm_scale, 'W_out': W_out}
    _L0_attn_in = _L0_attn_setup()

    def _L0_ffn_setup():
        import jax, jax.numpy as jnp
        import numpy as np
        K = 2

        def gelu(v):
            return jax.nn.gelu(v, approximate=False)
        key = jax.random.key(seed)
        ks = jax.random.split(key, 10)
        B, S, D, H, E = (4, 512, 512, 256, 8)
        SH = 2 * H
        u = lambda k_, shape, b: jax.random.uniform(k_, shape, jnp.float32, -b, b)
        return {'x': jax.random.normal(ks[0], (B, S, D), jnp.float32), 'gate_w': u(ks[1], (D, E), 1.0 / D), 'w1': u(ks[2], (E, D, H), 1.0 / D), 'b1': u(ks[3], (E, H), 1.0 / np.sqrt(D)), 'w2': u(ks[4], (E, H, D), 1.0 / H), 'b2': u(ks[5], (E, D), 1.0 / np.sqrt(H)), 'shared_w1': u(ks[6], (D, SH), 1.0 / D), 'shared_b1': u(ks[7], (SH,), 1.0 / np.sqrt(D)), 'shared_w2': u(ks[8], (SH, D), 1.0 / SH), 'shared_b2': u(ks[9], (D,), 1.0 / np.sqrt(SH))}
    _L0_ffn_in = _L0_ffn_setup()
    _d = {'L0_attn_x': _L0_attn_in['x'], 'L0_attn_W_mem': _L0_attn_in['W_mem'], 'L0_attn_conv_k': _L0_attn_in['conv_k'], 'L0_attn_W_q': _L0_attn_in['W_q'], 'L0_attn_theta': _L0_attn_in['theta'], 'L0_attn_decay_slopes': _L0_attn_in['decay_slopes'], 'L0_attn_anchor_slopes': _L0_attn_in['anchor_slopes'], 'L0_attn_score_scale': _L0_attn_in['score_scale'], 'L0_attn_W_re': _L0_attn_in['W_re'], 'L0_attn_W_im': _L0_attn_in['W_im'], 'L0_attn_norm_scale': _L0_attn_in['norm_scale'], 'L0_attn_W_out': _L0_attn_in['W_out'], 'L0_ffn_gate_w': _L0_ffn_in['gate_w'], 'L0_ffn_w1': _L0_ffn_in['w1'], 'L0_ffn_b1': _L0_ffn_in['b1'], 'L0_ffn_w2': _L0_ffn_in['w2'], 'L0_ffn_b2': _L0_ffn_in['b2'], 'L0_ffn_shared_w1': _L0_ffn_in['shared_w1'], 'L0_ffn_shared_b1': _L0_ffn_in['shared_b1'], 'L0_ffn_shared_w2': _L0_ffn_in['shared_w2'], 'L0_ffn_shared_b2': _L0_ffn_in['shared_b2']}
    _x0 = _d['L0_attn_x']
    _d['L0_attn_x'] = jax.random.normal(jax.random.fold_in(jax.random.key(seed), 1), (4, 512, 512), dtype=_x0.dtype)
    del _x0
    return _d

def reference(L0_attn_x, L0_attn_W_mem, L0_attn_conv_k, L0_attn_W_q, L0_attn_theta, L0_attn_decay_slopes, L0_attn_anchor_slopes, L0_attn_score_scale, L0_attn_W_re, L0_attn_W_im, L0_attn_norm_scale, L0_attn_W_out, L0_ffn_gate_w, L0_ffn_w1, L0_ffn_b1, L0_ffn_w2, L0_ffn_b2, L0_ffn_shared_w1, L0_ffn_shared_b1, L0_ffn_shared_w2, L0_ffn_shared_b2):

    def _L0_attn_ref(x, W_mem, conv_k, W_q, theta, decay_slopes, anchor_slopes, score_scale, W_re, W_im, norm_scale, W_out):
        import jax, jax.numpy as jnp
        import numpy as np
        from jax import lax
        B, L, D = (2, 1024, 512)
        K, KQ, M, H = (32, 4, 8, 8)
        MEM = K * H
        FLAT = K * H * M
        CONV_W = 4
        DIM_SWIGLU = H * 3 * 2
        N_DECAY = K - 4

        def _forward(x, W_mem, conv_k, W_q, theta, decay_slopes, anchor_slopes, score_scale, W_re, W_im, norm_scale, W_out):
            b, l, d = x.shape
            z = x @ W_mem
            z = lax.conv_general_dilated(z, conv_k, window_strides=(1,), padding=[(CONV_W - 1, 0)], dimension_numbers=('NHC', 'HIO', 'NHC'), feature_group_count=MEM + K)
            k_val = z[..., :MEM].reshape(b, l, K, H)
            s_raw = z[..., MEM:].reshape(b, l, K, 1)
            q = (x @ W_q).reshape(b, l, KQ, H, M, 2)
            q_re, q_im = (q[..., 0], q[..., 1])
            pos = jnp.arange(l, dtype=jnp.float32)
            slopes_d = jax.nn.softplus(decay_slopes).reshape(1, 1, -1, 1)
            slopes_a = jax.nn.softplus(anchor_slopes).reshape(1, 1, -1, 1)
            dist = jnp.maximum(jnp.float32(l - 1) - pos, 0.0)
            log_w = jnp.concatenate([-slopes_d * dist[None, :, None, None], -slopes_a * pos[None, :, None, None]], axis=2)
            log_p = jnp.clip(score_scale[None, None, :, None] * s_raw, -20.0, 20.0)
            p_w = jnp.exp(log_p + log_w)
            phi = k_val[..., None] * theta
            re_k, im_k = (jnp.cos(phi), jnp.sin(phi))
            pw5 = p_w[..., None]
            merged = jnp.concatenate([p_w.squeeze(-1), (pw5 * re_k).reshape(b, l, FLAT), (pw5 * im_k).reshape(b, l, FLAT)], axis=-1)
            cs = jnp.cumsum(merged, axis=1)
            den = cs[..., :K]
            num_re = cs[..., K:K + FLAT]
            num_im = cs[..., K + FLAT:]
            inv_den = 1.0 / jnp.maximum(den[..., None], 0.0001)
            state_re = num_re.reshape(b, l, K, H, M) * inv_den[..., None]
            state_im = num_im.reshape(b, l, K, H, M) * inv_den[..., None]
            n_rep = K // KQ
            q_re = jnp.repeat(q_re, n_rep, axis=2)
            q_im = jnp.repeat(q_im, n_rep, axis=2)
            out_re = jnp.sum(state_re * q_re + state_im * q_im, axis=-1)
            out_im = jnp.sum(state_im * q_re - state_re * q_im, axis=-1)
            out_re = out_re * norm_scale
            out_im = out_im * norm_scale
            y = jnp.einsum('blkh,khn->blkn', out_re, W_re) + jnp.einsum('blkh,khn->blkn', out_im, W_im)
            y_val, y_gate = jnp.split(y, 2, axis=-1)
            y = (y_val * jax.nn.silu(y_gate)).reshape(b, l, -1)
            return y @ W_out
        return _forward(x, W_mem, conv_k, W_q, theta, decay_slopes, anchor_slopes, score_scale, W_re, W_im, norm_scale, W_out)

    def _L0_ffn_ref(x, gate_w, w1, b1, w2, b2, shared_w1, shared_b1, shared_w2, shared_b2):
        import jax, jax.numpy as jnp
        import numpy as np
        K = 2

        def gelu(v):
            return jax.nn.gelu(v, approximate=False)
        B, S, D = x.shape
        E = gate_w.shape[1]
        xf = x.reshape(-1, D)
        logits = xf @ gate_w
        top_logits, top_idx = jax.lax.top_k(logits, K)
        top_gates = jax.nn.softmax(top_logits, axis=-1)
        gates = jnp.sum(jax.nn.one_hot(top_idx, E, dtype=xf.dtype) * top_gates[..., None], axis=1)
        h = gelu(jnp.einsum('nd,edh->neh', xf, w1) + b1)
        out_e = jnp.einsum('neh,ehd->ned', h, w2) + b2
        routed = jnp.einsum('ne,ned->nd', gates, out_e)
        shared = gelu(xf @ shared_w1 + shared_b1) @ shared_w2 + shared_b2
        return (routed + shared).reshape(B, S, D)
    x = L0_attn_x
    x = x + 0.5 * _L0_ffn_ref(_layernorm(x, axis=-1), L0_ffn_gate_w, L0_ffn_w1, L0_ffn_b1, L0_ffn_w2, L0_ffn_b2, L0_ffn_shared_w1, L0_ffn_shared_b1, L0_ffn_shared_w2, L0_ffn_shared_b2)
    x = x + _L0_attn_ref(_layernorm(x, axis=-1), L0_attn_W_mem, L0_attn_conv_k, L0_attn_W_q, L0_attn_theta, L0_attn_decay_slopes, L0_attn_anchor_slopes, L0_attn_score_scale, L0_attn_W_re, L0_attn_W_im, L0_attn_norm_scale, L0_attn_W_out)
    x = x + 0.5 * _L0_ffn_ref(_layernorm(x, axis=-1), L0_ffn_gate_w, L0_ffn_w1, L0_ffn_b1, L0_ffn_w2, L0_ffn_b2, L0_ffn_shared_w1, L0_ffn_shared_b1, L0_ffn_shared_w2, L0_ffn_shared_b2)
    return x

_drawn_inputs = setup_inputs


def setup_inputs(seed=0):
    import zlib

    import numpy as np

    out = dict(_drawn_inputs(seed))
    spreads = {'L0_attn_score_scale': (1.0, 0.6), 'L0_attn_norm_scale': (1.0, 0.2)}
    factors = {'L0_ffn_gate_w': 3.769,
     'L0_ffn_w1': 29.089,
     'L0_ffn_b1': 29.73,
     'L0_ffn_w2': 8.0,
     'L0_ffn_b2': 3.142,
     'L0_ffn_shared_w1': 29.065,
     'L0_ffn_shared_b1': 28.931,
     'L0_ffn_shared_w2': 8.0,
     'L0_ffn_shared_b2': 2.953}
    for name, (base, spread) in spreads.items():
        noise = np.random.default_rng([zlib.crc32(name.encode()), seed]).standard_normal(out[name].shape)
        drawn = base * np.exp(spread * noise) if base else spread * noise
        out[name] = jnp.asarray(drawn.astype(out[name].dtype))
    for name, factor in factors.items():
        out[name] = (out[name] * factor).astype(out[name].dtype)
    return out
```

```python
import math
from contextlib import ExitStack

import numpy as np

import concourse.bass as bass
from concourse import mybir
from concourse.alu_op_type import AluOpType as ALU

F32 = mybir.dt.float32
I32 = mybir.dt.int32
ACT = mybir.ActivationFunctionType
AX = mybir.AxisListType

P = 128
TWO_PI = 6.283185


class Line:

    def __init__(self, sem):
        self.sem, self.value = sem, 0

    def mark(self, instruction, by=1):
        instruction.then_inc(self.sem, by)
        self.value += by
        return (self, self.value)


class Waits:

    def __init__(self):
        self.passed = {}

    def need(self, engine, *points):
        for point in points:
            if point is None:
                continue
            line, value = point
            key = (id(engine), id(line))
            if self.passed.get(key, 0) < value:
                engine.wait_ge(line.sem, value)
                self.passed[key] = value


def macaron(nc, x, w_mem, conv_k, w_q, theta, decay, anchor, score_scale, w_re, w_im, norm_scale,
            w_out, gate_w, w1, b1, w2, b2, sw1, sb1, sw2, sb2, out):
    B, T, D = x.shape
    E, _, H = w1.shape
    SH = sw1.shape[1]
    K, HH, N2 = w_re.shape
    M = theta.shape[4]
    KQ = w_q.shape[1] // (HH * M * 2)
    CW = conv_k.shape[0]
    KH = K * HH
    KC = D // P
    TB = T // P
    HALVES = KH // P
    EC = H // P
    SC = SH // P
    NV = N2 // 2
    VT = K * NV // P
    VH = VT // HALVES
    ND = decay.shape[0]
    KPQ = K // KQ
    KT = P // HH
    QH = KQ // HALVES
    assert (P, T, D) == (128, 512, 512) and HH * M * 2 == P and K == 32 and CW == 4

    ctx = ExitStack()
    with ctx:
        def sb(name, shape, dt=F32):
            return ctx.enter_context(nc.sbuf_tensor(name, shape, dt))

        def line(name):
            return Line(ctx.enter_context(nc.semaphore(name)))

        w1_sb = sb("w1_sb", [P, E, KC, H])
        w2_sb = sb("w2_sb", [P, E * EC, D])
        sw1_sb = sb("sw1_sb", [P, KC, SH])
        sw2_sb = sb("sw2_sb", [P, SC, D])
        gate_sb = sb("gate_sb", [P, KC, E])
        b1_sb = sb("b1_sb", [P, E * EC])
        sb1_sb = sb("sb1_sb", [P, SC])
        wmem_sb = sb("wmem_sb", [P, KC, KH + K])
        wq_sb = sb("wq_sb", [P, KC, KQ, 2, M, HH])
        wbd_sb = sb("wbd_sb", [P, HALVES, 2, 2, KT, NV])
        wout_sb = sb("wout_sb", [P, VT, D])
        conv_sb = sb("conv_sb", [P, HALVES + 1, CW])
        theta_sb = sb("theta_sb", [P, HALVES, M])
        norm_sb = sb("norm_sb", [P, HALVES])
        scale_sb = sb("scale_sb", [K, 1])
        G0 = 2 * K
        low_rows = sb("low_rows", [P, T])
        logw_sb = low_rows[0:K, :]
        b2_sb = low_rows[G0:G0 + E + 1, :]
        ident = sb("ident", [P, P])
        rep_sb = sb("rep_sb", [K, KH])
        before = sb("before", [P, E, E])
        minus_half = sb("minus_half", [P, TB])
        half_pi = sb("half_pi", [P, 1])
        zero1 = sb("zero1", [P, 1])
        slope = sb("slope", [K, 8])

        xin = sb("xin", [P, TB, D])
        stats = sb("stats", [P, TB, 6])
        mv = sb("mv", [P, TB, 2])
        rstd = sb("rstd", [P, 3, TB])
        xnT = sb("xnT", [P, KC, T])
        NHB = 3
        hT = sb("hT", [P, NHB, T])
        NGB = 2
        gateT = sb("gateT", [P, NGB, T])
        lg = sb("lg", [P, TB, E])
        cmp_a = sb("cmp_a", [P, TB, E, E])
        cmp_b = sb("cmp_b", [P, TB, E, E])
        rank = sb("rank", [P, TB, E])
        top = sb("top", [P, TB])
        ge = sb("ge", [P, TB, E])
        g9 = sb("g9", [P, TB, E + 1])
        NRES = 2
        res = sb("res", [P, NRES, D])

        kval = sb("kval", [P, HALVES, T])
        pwx = sb("pwx", [P, HALVES, T])
        invx = sb("invx", [P, HALVES, T])
        high_rows = sb("high_rows", [P, 2, T])
        pw = high_rows[0:K, :, :]
        gT = high_rows[G0:G0 + E + 1, 0, :]
        outT = sb("outT", [P, HALVES, 2, T])
        NQX = 2
        qx = sb("qx", [P, NQX, 2, T])
        core = sb("core", [P, 20 * 256])
        turn = core[:, 0:2 * T].rearrange("p (s t) -> p s t", s=2)
        trig = core[:, 2 * T:6 * T].rearrange("p (s c t) -> p s c t", s=2, c=2)
        run = core[:, 6 * T:8 * T].rearrange("p (c t) -> p c t", c=2)
        prod = core[:, 8 * T:10 * T].rearrange("p (c t) -> p c t", c=2)
        anT = core[:, 2 * T:6 * T].rearrange("p (c t) -> p c t", c=KC)
        ZP = T + CW - 1
        zT = core[:, 6 * T:6 * T + 2 * 516].rearrange("p (s t) -> p s t", s=2)
        qT = core[:, 0:2 * T].rearrange("p (s t) -> p s t", s=2)
        yT = core[:, 0:VT * T].rearrange("p (v t) -> p v t", v=VT)
        sil = core[:, VT * T:(VT + 2) * T].rearrange("p (s t) -> p s t", s=2)

        acc = ctx.enter_context(nc.psum_tensor("acc", [P, TB, D], F32))
        hps = ctx.enter_context(nc.psum_tensor("hps", [P, 2, T], F32))
        misc = ctx.enter_context(nc.psum_tensor("misc", [P, 2, T], F32))

        x1_dram = nc.dram_tensor("x1_rows", (B, T, D), F32).ap()
        x2_dram = nc.dram_tensor("x2_rows", (B, T, D), F32).ap()
        q_dram = nc.dram_tensor("q_cols", (KQ, M, HH, 2, T), F32)
        g_dram = nc.dram_tensor("gate_cols", (E + 1, T), F32)

        pe, act, dve, pool = line("s_pe"), line("s_act"), line("s_dve"), line("s_pool")
        l_xin = line("s_xin")
        l_res = [line(f"s_res{i}") for i in range(NRES)]
        l_gst = line("s_gate_store")
        l_gate = [line(f"s_gate{i}") for i in range(NGB)]
        l_qst = [line(f"s_q_store{i}") for i in range(2)]
        l_qx = [line(f"s_qx{i}") for i in range(NQX)]
        l_w1 = line("s_w1")
        l_const = line("s_const")
        l_attn = line("s_attn_weights")
        l_expert = [line(f"s_expert{e}") for e in range(E)]
        lines = [pe, act, dve, pool, l_xin, *l_res, l_gst, *l_gate, *l_qst, *l_qx, l_w1, l_const,
                 l_attn, *l_expert]

        PE, VE, SE, GE, SP = nc.tensor, nc.vector, nc.scalar, nc.gpsimd, nc.sync
        waits = Waits()
        need = waits.need
        free = {}
        turns = {}

        def take(name, n):
            i = turns.get(name, 0)
            turns[name] = i + 1
            return i % n

        def section_end():
            for ln in lines:
                need(SP, (ln, ln.value))
            nc.all_engine_barrier()
            nums = [ln.sem for ln in lines]
            for s in nums:
                GE.sem_clear(s)
            nc.all_engine_barrier()
            for ln in lines:
                ln.value = 0
            waits.passed.clear()
            free.clear()
            turns.clear()

        def rows(dram, b):
            return bass.AP(dram.tensor, dram.offset + b * (T * D), [[D, P], [P * D, TB], [1, D]])

        def row_tile(dram, b, tb):
            return bass.AP(dram.tensor, dram.offset + b * (T * D) + tb * P * D, [[D, P], [1, D]])

        def layernorm_T(src, b, dst, dst_free):
            need(SP, free.get("xin"))
            loaded = l_xin.mark(SP.dma_start(xin[:, :, :], rows(src, b)), 16)
            need(VE, loaded)
            for tb in range(TB):
                s = dve.mark(VE.bn_stats(stats[:, tb, :], xin[:, tb, :]))
            need(VE, s)
            for tb in range(TB):
                s = dve.mark(VE.bn_aggr(mv[:, tb, :], stats[:, tb, :]))
            need(GE, s)
            r, v, u = rstd[:, 0, :], rstd[:, 1, :], rstd[:, 2, :]
            need(GE, pool.mark(GE.tensor_scalar(v, mv[:, :, 1], 1e-5, None, ALU.add)))
            need(GE, pool.mark(GE.tensor_tensor(r, v, minus_half[:, :], ALU.pow)))
            need(GE, pool.mark(GE.tensor_tensor(u, r, r, ALU.mult)))
            need(GE, pool.mark(GE.tensor_tensor(u, u, v, ALU.mult)))
            need(GE, pool.mark(GE.tensor_scalar(u, u, -0.5, 1.5, ALU.mult, ALU.add)))
            s = pool.mark(GE.tensor_tensor(r, r, u, ALU.mult))
            need(VE, s)
            for tb in range(TB):
                s = dve.mark(VE.tensor_scalar(xin[:, tb, :], xin[:, tb, :], mv[:, tb, 0:1],
                                              rstd[:, 0, tb:tb + 1], ALU.subtract, ALU.mult))
                bank = take("misc", 2)
                need(PE, s, free.get(("misc", bank)))
                for c in range(KC):
                    t = PE.transpose(misc[:, bank, c * P:(c + 1) * P], xin[:, tb, c * P:(c + 1) * P],
                                     ident[:, :])
                t = pe.mark(t)
                free["xin"] = t
                need(SE, t, *dst_free)
                s = act.mark(SE.copy(dst[:, :, tb * P:(tb + 1) * P],
                                     misc[:, bank, :].rearrange("p (c t) -> p c t", c=KC)))
                free["misc", bank] = s
            return s

        def gates(xn_ready):
            bank = take("misc", 2)
            need(PE, xn_ready, free.get(("misc", bank)))
            for tb in range(TB):
                for c in range(KC):
                    t = PE.matmul(misc[:, bank, tb * E:(tb + 1) * E], xnT[:, c, tb * P:(tb + 1) * P],
                                  gate_sb[:, c, :], start=c == 0, stop=c == KC - 1)
            need(VE, pe.mark(t))
            s = dve.mark(VE.tensor_copy(lg[:, :, :],
                                        misc[:, bank, 0:TB * E].rearrange("p (t e) -> p t e", e=E)))
            free["misc", bank] = s
            need(VE, s)
            other = lg[:, :, None, :].broadcast_to([P, TB, E, E])
            own = lg[:, :, :, None].broadcast_to([P, TB, E, E])
            low = before[:, None, :, :].broadcast_to([P, TB, E, E])
            dve.mark(VE.tensor_tensor(cmp_a[:, :, :, :], other, own, ALU.is_gt))
            dve.mark(VE.tensor_reduce(top[:, :], lg[:, :, :], AX.X, ALU.max))
            need(VE, dve.mark(VE.tensor_tensor(cmp_b[:, :, :, :], other, own, ALU.is_equal)))
            need(VE, dve.mark(VE.tensor_tensor(cmp_b[:, :, :, :], cmp_b[:, :, :, :], low, ALU.mult)))
            s = dve.mark(VE.tensor_tensor(ge[:, :, :], lg[:, :, :],
                                          top[:, :, None].broadcast_to([P, TB, E]), ALU.subtract))
            need(SE, s)
            e = act.mark(SE.activation(ge[:, :, :], ge[:, :, :], ACT.Exp))
            need(VE, dve.mark(VE.tensor_tensor(cmp_a[:, :, :, :], cmp_a[:, :, :, :],
                                               cmp_b[:, :, :, :], ALU.add)))
            need(VE, dve.mark(VE.tensor_reduce(rank[:, :, :], cmp_a[:, :, :, :], AX.X, ALU.add)))
            need(VE, dve.mark(VE.tensor_scalar(rank[:, :, :], rank[:, :, :], 1.5, None, ALU.is_lt)))
            need(VE, e)
            need(VE, dve.mark(VE.tensor_tensor(ge[:, :, :], ge[:, :, :], rank[:, :, :], ALU.mult)))
            need(VE, dve.mark(VE.tensor_reduce(top[:, :], ge[:, :, :], AX.X, ALU.add)))
            need(VE, dve.mark(VE.reciprocal(top[:, :], top[:, :])))
            s = dve.mark(VE.tensor_tensor(g9[:, :, 0:E], ge[:, :, :],
                                          top[:, :, None].broadcast_to([P, TB, E]), ALU.mult))
            bank = take("misc", 2)
            need(PE, s, free.get(("misc", bank)))
            for tb in range(TB):
                t = PE.transpose(misc[0:E + 1, bank, tb * P:(tb + 1) * P], g9[:, tb, :], ident[:, :])
            t = pe.mark(t)
            need(VE, t, free.get("gT"))
            gT_ready = dve.mark(VE.tensor_copy(gT[:, :], misc[0:E + 1, bank, :]))
            free["misc", bank] = gT_ready
            need(SP, gT_ready, free.get("g_dram"))
            stored = l_gst.mark(SP.dma_start(g_dram.ap(), gT[:, :]), 16)
            return gT_ready, stored

        def ffn(src, dst, b):
            xn_ready = layernorm_T(src, b, xnT, [free.get("xnT")])
            yield 3.0
            tiles = [("shared", j) for j in range(SC)] + [("routed", j) for j in range(E * EC)]
            gT_ready = stored = None
            gate_of = {}
            pending = None

            def accumulate(n, kind, j, slot, ready):
                w = sw2_sb[:, j, :] if kind == "shared" else w2_sb[:, j, :]
                need(PE, ready)
                if kind == "routed":
                    need(PE, (l_expert[j // EC], l_expert[j // EC].value))
                else:
                    need(PE, (l_w1, l_w1.value))
                if n == 0:
                    need(PE, free.get("acc"))
                last = n == len(tiles) - 1
                for tb in range(TB):
                    t = PE.matmul(acc[:, tb, :], hT[:, slot, tb * P:(tb + 1) * P], w,
                                  start=n == 0, stop=last)
                free["hT", slot] = pe.mark(t)
                return free["hT", slot]

            for n, (kind, j) in enumerate(tiles):
                if n == 1:
                    gT_ready, stored = gates(xn_ready)
                if kind == "routed" and j % EC == 0:
                    e = j // EC
                    g = take("gateT", NGB)
                    need(SP, stored, free.get(("gateT", g)))
                    gate_of[e] = (g, l_gate[g].mark(
                        SP.dma_start(gateT[:, g, :], bass.AP(g_dram, e * T, [[0, P], [1, T]])), 16))
                    free["g_dram"] = gate_of[e][1]
                bank = take("hps", 2)
                need(PE, xn_ready, free.get(("hps", bank)))
                if kind == "shared":
                    need(PE, (l_w1, l_w1.value))
                else:
                    need(PE, (l_expert[j // EC], l_expert[j // EC].value))
                for c in range(KC):
                    if kind == "shared":
                        w = sw1_sb[:, c, j * P:(j + 1) * P]
                    else:
                        w = w1_sb[:, j // EC, c, (j % EC) * P:(j % EC + 1) * P]
                    t = PE.matmul(hps[:, bank, :], w, xnT[:, c, :], start=c == 0, stop=c == KC - 1)
                t = pe.mark(t)
                free["xnT"] = t
                slot = take("hT", NHB)
                need(SE, t, free.get(("hT", slot)))
                bias = sb1_sb[:, j:j + 1] if kind == "shared" else b1_sb[:, j:j + 1]
                ready = act.mark(SE.activation(hT[:, slot, :], hps[:, bank, :], ACT.Gelu, bias=bias))
                free["hps", bank] = ready
                if kind == "routed":
                    g, there = gate_of[j // EC]
                    need(VE, ready, there)
                    ready = dve.mark(VE.tensor_tensor(hT[:, slot, :], hT[:, slot, :],
                                                      gateT[:, g, :], ALU.mult))
                    free["gateT", g] = ready
                if pending is not None:
                    accumulate(*pending)
                pending = (n, kind, j, slot, ready)
                if kind == "routed" and j == 0:
                    need(PE, gT_ready)
                    for tb in range(TB):
                        t = PE.matmul(acc[:, tb, :], gT[:, tb * P:(tb + 1) * P], b2_sb[:, :],
                                      start=False, stop=False)
                    free["gT"] = pe.mark(t)
                yield 6.8
            done = accumulate(*pending)
            for tb in range(TB):
                store_rows(src, dst, b, tb, acc[:, tb, :], done, 0.5)
                free["acc"] = (dve, dve.value)
            yield 1.0

        def store_rows(src, dst, b, tb, result, ready, factor):
            s = take("res", NRES)
            need(SP, free.get(("res", s)))
            loaded = l_res[s].mark(SP.dma_start(res[:, s, :], row_tile(src, b, tb)), 16)
            need(VE, ready, loaded)
            summed = dve.mark(VE.scalar_tensor_tensor(res[:, s, :], result, factor, res[:, s, :],
                                                      ALU.mult, ALU.add))
            need(SP, summed)
            free["res", s] = l_res[s].mark(SP.dma_start(row_tile(dst, b, tb), res[:, s, :]), 16)
            return summed

        def attention_inputs(b):
            an_ready = layernorm_T(x1_dram, b, anT, [])
            need(PE, (l_attn, l_attn.value))
            conv_done = {}
            for i in range(HALVES + 1):
                rowsn = P if i < HALVES else K
                bank = take("misc", 2)
                need(PE, an_ready, free.get(("misc", bank)))
                for c in range(KC):
                    t = PE.matmul(misc[0:rowsn, bank, :], wmem_sb[:, c, i * P:i * P + rowsn],
                                  anT[:, c, :], start=c == 0, stop=c == KC - 1)
                z = zT[0:rowsn, i % 2, :]
                need(SE, pe.mark(t), conv_done.get(i - 2))
                if i < 2:
                    need(VE, dve.mark(VE.memset(z[:, 0:CW - 1], 0.0)))
                s = act.mark(SE.copy(z[:, CW - 1:ZP], misc[0:rowsn, bank, :]))
                free["misc", bank] = s
                need(VE, s)
                o = kval[:, i, :] if i < HALVES else pw[:, 0, :]
                s = dve.mark(VE.tensor_scalar(o, z[:, 0:T], conv_sb[0:rowsn, i, 0:1], None, ALU.mult))
                for k in range(1, CW):
                    need(VE, s)
                    s = dve.mark(VE.scalar_tensor_tensor(o, z[:, k:k + T],
                                                         conv_sb[0:rowsn, i, k:k + 1], o,
                                                         ALU.mult, ALU.add))
                conv_done[i] = s
            need(VE, s)
            p, den = pw[:, 0, :], pw[:, 1, :]
            need(VE, dve.mark(VE.tensor_scalar(p, p, scale_sb[:, 0:1], 20.0, ALU.mult, ALU.min)))
            s = dve.mark(VE.scalar_tensor_tensor(p, p, -20.0, logw_sb[:, :], ALU.max, ALU.add))
            need(SE, s)
            s = act.mark(SE.activation(p, p, ACT.Exp))
            need(VE, s)
            need(VE, dve.mark(VE.tensor_tensor_scan(den, p, zero1[0:K, 0:1].broadcast_to([K, T]), 0.0,
                                                    ALU.add, ALU.add)))
            need(VE, dve.mark(VE.tensor_scalar(den, den, 1e-4, None, ALU.max)))
            den_ready = dve.mark(VE.reciprocal(den, den))
            for q in range(KQ):
                bank = take("misc", 2)
                need(PE, free.get(("misc", bank)))
                for c in range(KC):
                    t = PE.matmul(misc[:, bank, :], wq_sb[:, c, q, :, :, :].rearrange("p a b c -> p (a b c)"),
                                  anT[:, c, :], start=c == 0, stop=c == KC - 1)
                t = pe.mark(t)
                free["anT"] = t
                need(SE, t, free.get(("qT", q % 2)))
                s = act.mark(SE.copy(qT[:, q % 2, :], misc[:, bank, :]))
                free["misc", bank] = s
                need(SP, s)
                free["qT", q % 2] = l_qst[q % 2].mark(
                    SP.dma_start(bass.AP(q_dram, q * P * T, [[T, 2], [2 * T, M * HH], [1, T]]), qT[:, q % 2, :]), 16)
            for i, dst in enumerate((pwx, invx)):
                for half in range(HALVES):
                    bank = take("misc", 2)
                    need(PE, den_ready, free.get(("misc", bank)))
                    t = pe.mark(PE.matmul(misc[:, bank, :], rep_sb[:, half * P:(half + 1) * P],
                                          pw[:, i, :], start=True, stop=True))
                    need(SE, t)
                    s = act.mark(SE.copy(dst[:, half, :], misc[:, bank, :]))
                    free["misc", bank] = s
            return s

        def attention_core(b, spread_ready):
            steps = [(half, m) for half in range(HALVES) for m in range(M)]
            front = {}

            def load_queries(n):
                half, m = steps[n]
                s = n % NQX
                need(SP, free.get(("qx", s)), *[(ln, ln.value) for ln in l_qst])
                for g in range(QH):
                    q = half * QH + g
                    src = bass.AP(q_dram, q * P * T + m * HH * 2 * T,
                                  [[0, KPQ], [2 * T, HH], [1, 2 * T]])
                    at = l_qx[s].mark(SP.dma_start(qx[g * KPQ * HH:(g + 1) * KPQ * HH, s, :, :], src), 16)
                front[n, "q"] = at

            def phases(n):
                half, m = steps[n]
                s = n % 2
                f, nearest = turn[:, s, :], prod_int(s)
                th = theta_sb[:, half, m:m + 1]
                need(VE, free.get(("turn", s)), *[(ln, ln.value) for ln in l_qst])
                r = dve.mark(VE.tensor_scalar(nearest, kval[:, half, :], th, None, ALU.mult))
                need(VE, r)
                r = dve.mark(VE.scalar_tensor_tensor(f, kval[:, half, :], th, nearest,
                                                     ALU.mult, ALU.subtract))
                need(SE, r, free.get(("trig", s)), free.get("anT"))
                a = act.mark(SE.activation(trig[:, s, 0, :], f, ACT.Abs))
                act.mark(SE.activation(trig[:, s, 1, :], f, ACT.Sin, scale=TWO_PI))
                need(SE, a)
                a = act.mark(SE.activation(trig[:, s, 0, :], trig[:, s, 0, :], ACT.Sin,
                                           scale=-TWO_PI, bias=half_pi[:, 0:1]))
                free["turn", s] = a
                front[n] = a

            def prod_int(s):
                return turn[:, s, :].bitcast(I32)

            def sums(n):
                half, m = steps[n]
                s, qs = n % 2, n % NQX
                cs = trig[:, s, :, :]
                need(VE, front[n], spread_ready)
                w = dve.mark(VE.tensor_tensor(cs, cs, pwx[:, half, None, :].broadcast_to([P, 2, T]),
                                              ALU.mult))
                need(VE, w)
                for c in range(2):
                    w = dve.mark(VE.tensor_tensor_scan(run[:, c, :], trig[:, s, c, :],
                                                       zero1[:, 0:1].broadcast_to([P, T]), 0.0,
                                                       ALU.add, ALU.add))
                free["trig", s] = w
                need(VE, w, front[n, "q"])
                w = dve.mark(VE.tensor_tensor(prod[:, :, :], run[:, :, :], qx[:, qs, :, :], ALU.mult))
                need(VE, w)
                back = bass.AP(run.tensor, run.offset + T, [list(run.ap[0]), [-T, 2], [1, T]])
                w3 = dve.mark(VE.tensor_tensor(qx[:, qs, :, :], back, qx[:, qs, :, :], ALU.mult))
                re, im = outT[:, half, 0, :], outT[:, half, 1, :]
                need(VE, w3)
                if m == 0:
                    w = dve.mark(VE.tensor_tensor(re, prod[:, 0, :], prod[:, 1, :], ALU.add))
                    w3 = dve.mark(VE.tensor_tensor(im, qx[:, qs, 0, :], qx[:, qs, 1, :], ALU.subtract))
                else:
                    w = dve.mark(VE.tensor_tensor(prod[:, 0, :], prod[:, 0, :], prod[:, 1, :], ALU.add))
                    w3 = dve.mark(VE.tensor_tensor(qx[:, qs, 0, :], qx[:, qs, 0, :], qx[:, qs, 1, :],
                                                   ALU.subtract))
                    need(VE, w)
                    dve.mark(VE.tensor_tensor(re, re, prod[:, 0, :], ALU.add))
                    need(VE, w3)
                    w3 = dve.mark(VE.tensor_tensor(im, im, qx[:, qs, 0, :], ALU.add))
                free["qx", qs] = w3
                if m == M - 1:
                    for part in range(2):
                        need(VE, (dve, dve.value))
                        o = outT[:, half, part, :]
                        w3 = dve.mark(VE.scalar_tensor_tensor(o, o, norm_sb[:, half:half + 1],
                                                              invx[:, half, :], ALU.mult, ALU.mult))
                    free["outT", half] = w3

            load_queries(0)
            phases(0)
            for n in range(len(steps)):
                if n + 1 < len(steps):
                    load_queries(n + 1)
                    phases(n + 1)
                yield 4.5
                sums(n)
                yield 4.5

        def attention_output(b):
            yT_ready = []
            core_done = (dve, dve.value)
            for v in range(VT):
                half, j = v // VH, v % VH
                banks = []
                for vg in range(2):
                    bank = take("misc", 2)
                    banks.append(bank)
                    need(PE, free["outT", half], free.get(("misc", bank)))
                    for part in range(2):
                        w = wbd_sb[:, half, part, vg, :, :].rearrange("p k n -> p (k n)")
                        t = PE.matmul(misc[:, bank, :], w[:, j * P:(j + 1) * P],
                                      outT[:, half, part, :], start=part == 0, stop=part == 1)
                    t = pe.mark(t)
                need(SE, t, core_done, free.get(("sil", v % 2)))
                s = act.mark(SE.activation(sil[:, v % 2, :], misc[:, banks[1], :], ACT.Silu))
                free["misc", banks[1]] = s
                need(VE, s)
                s = dve.mark(VE.tensor_tensor(yT[:, v, :], misc[:, banks[0], :], sil[:, v % 2, :],
                                              ALU.mult))
                free["misc", banks[0]] = s
                free["sil", v % 2] = s
                yield 3.4
            for tb in range(TB):
                bank = take("misc", 2)
                need(PE, s, free.get(("misc", bank)))
                for v in range(VT):
                    t = PE.matmul(misc[:, bank, :], yT[:, v, tb * P:(tb + 1) * P], wout_sb[:, v, :],
                                  start=v == 0, stop=v == VT - 1)
                free["misc", bank] = store_rows(x1_dram, x2_dram, b, tb, misc[:, bank, :],
                                                pe.mark(t), 1.0)
                yield 5.1

        def chain(*parts):
            for p in parts:
                yield from p

        def together(a, f):
            ta = tf = 0.0
            live = [a, f]
            while live:
                g = live[0] if len(live) == 1 else (a if ta <= tf else f)
                try:
                    c = next(g)
                except StopIteration:
                    live.remove(g)
                    continue
                if g is a:
                    ta += c
                else:
                    tf += c

        def section(b, second_ffn, first_ffn):
            spread = attention_inputs(b)
            others = []
            if second_ffn:
                others.append(ffn(x2_dram, out, b - 1))
            if first_ffn:
                others.append(ffn(x, x1_dram, b + 1))
            together(chain(attention_core(b, spread), attention_output(b)), chain(*others))
            section_end()

        def load(ln, dst, src, eng=SP):
            return ln.mark(eng.dma_start(dst, src), 16)

        nc_dma = nc.allow_non_contiguous_dma(reason="small bias and scale vectors, loaded once")
        ctx.enter_context(nc_dma)
        load(l_const, gate_sb[:, :, :], gate_w.rearrange("(c p) e -> p c e", p=P), SE)
        load(l_const, sb1_sb[:, :], sb1.rearrange("(c p) -> p c", p=P), SE)
        load(l_const, b1_sb[:, :], b1.rearrange("e (c p) -> p (e c)", p=P), SE)
        load(l_const, b2_sb[0:E, :], b2, SE)
        load(l_const, b2_sb[E:E + 1, :], sb2.rearrange("(a d) -> a d", a=1), SE)
        load(l_w1, sw1_sb[:, :, :], sw1.rearrange("(c p) h -> p c h", p=P), SE)
        load(l_w1, sw2_sb[:, :, :], sw2.rearrange("(c p) d -> p c d", p=P), SE)
        for e in range(E):
            load(l_expert[e], w1_sb[:, e, :, :], w1[e].rearrange("(c p) h -> p c h", p=P), SE)
            load(l_expert[e], w2_sb[:, e * EC:(e + 1) * EC, :], w2[e].rearrange("(c p) d -> p c d", p=P), SE)
        load(l_attn, theta_sb[:, :, :], theta.rearrange("a b (g k) h m -> (a b k h) g m", g=HALVES), SE)
        load(l_attn, norm_sb[:, :], norm_scale.rearrange("a b (g k) h -> (a b k h) g", g=HALVES), SE)
        for i in range(HALVES + 1):
            rowsn = P if i < HALVES else K
            load(l_attn, conv_sb[0:rowsn, i, :],
                 conv_k[:, 0, i * P:i * P + rowsn].rearrange("w p -> p w"), SE)
        load(l_attn, scale_sb[:, :], score_scale.rearrange("(p a) -> p a", a=1), SE)
        load(l_attn, slope[0:ND, 0:1], decay.rearrange("(p a) -> p a", a=1), SE)
        load(l_attn, slope[ND:K, 0:1], anchor.rearrange("(p a) -> p a", a=1), SE)
        load(l_attn, wmem_sb[:, :, :], w_mem.rearrange("(c p) n -> p c n", p=P), SE)
        wq_raw = core[:, 2 * T:2 * T + KC * KQ * P].rearrange("p (c n) -> p c n", c=KC)
        load(l_attn, wq_raw, w_q.rearrange("(c p) n -> p c n", p=P), SE)
        w_raw = core[:, 0:2 * HALVES * N2].rearrange("p (i g n) -> p i g n", i=2, g=HALVES)
        load(l_attn, w_raw[:, 0, :, :], w_re.rearrange("(g k) h n -> (k h) g n", g=HALVES), SE)
        load(l_attn, w_raw[:, 1, :, :], w_im.rearrange("(g k) h n -> (k h) g n", g=HALVES), SE)
        load(l_attn, wout_sb[:, :, :], w_out.rearrange("(v p) d -> p v d", p=P), SE)

        def pg(i):
            return pool.mark(i)

        pg(GE.memset(minus_half[:, :], -0.5))
        pg(GE.memset(half_pi[:, :], math.pi / 2))
        pg(GE.memset(zero1[:, :], 0.0))
        pg(GE.memset(g9[:, :, :], 1.0))
        pg(GE.memset(before[:, :, :], 1.0))
        pg(GE.memset(rep_sb[:, :], 1.0))
        need(GE, pg(GE.memset(ident[:, :], 0.0)))
        ident_ready = pg(GE.affine_select(out=ident[:, :], in_=ident[:, :], compare_op=ALU.not_equal,
                                          fill=1.0, base=0, pattern=[[-1, P]], channel_multiplier=1))
        pg(GE.affine_select(out=before[:, :, :], in_=before[:, :, :], compare_op=ALU.is_gt, fill=0.0,
                            base=0, pattern=[[1, E], [-1, E]], channel_multiplier=0))
        need(GE, pg(GE.affine_select(out=rep_sb[:, :], in_=rep_sb[:, :], compare_op=ALU.is_ge, fill=0.0,
                                     base=0, pattern=[[1, KH]], channel_multiplier=-HH)))
        consts = pg(GE.affine_select(out=rep_sb[:, :], in_=rep_sb[:, :], compare_op=ALU.is_ge, fill=0.0,
                                     base=HH - 1, pattern=[[-1, KH]], channel_multiplier=HH))

        need(PE, consts)
        need(VE, consts)
        need(SE, consts)
        for eng in (PE, SE, VE):
            need(eng, (l_const, l_const.value))
        for _ in ffn(x, x1_dram, 0):
            pass

        dist, posn = hT[0:K, 0, :], hT[0:K, 1, :]
        need(GE, (pe, pe.value))
        pg(GE.iota(dist, pattern=[[-1, T]], base=T - 1, channel_multiplier=0,
                   allow_small_or_imprecise_dtypes=True))
        need(GE, pg(GE.iota(posn, pattern=[[1, T]], base=0, channel_multiplier=0,
                            allow_small_or_imprecise_dtypes=True)))
        pg(GE.affine_select(out=dist, in_=dist, compare_op=ALU.is_gt, fill=0.0, base=ND,
                            pattern=[[0, T]], channel_multiplier=-1))
        dists = pg(GE.affine_select(out=posn, in_=posn, compare_op=ALU.is_ge, fill=0.0, base=-ND,
                                    pattern=[[0, T]], channel_multiplier=1))
        need(GE, (l_attn, l_attn.value))
        for half in range(HALVES):
            for part in range(2):
                for vg in range(2):
                    o = wbd_sb[:, half, part, vg, :, :]
                    i_ = w_raw[:, part, half, None, vg * NV:(vg + 1) * NV].broadcast_to([P, KT, NV])
                    need(GE, pg(GE.affine_select(out=o, in_=i_, compare_op=ALU.is_ge, fill=0.0, base=0,
                                                 pattern=[[-HH, KT], [0, NV]], channel_multiplier=1)))
                    wbd_ready = pg(GE.affine_select(out=o, in_=o, compare_op=ALU.is_ge, fill=0.0,
                                                    base=HH - 1, pattern=[[HH, KT], [0, NV]],
                                                    channel_multiplier=-1))
        need(VE, (l_attn, l_attn.value))
        for c in range(KC):
            for q in range(KQ):
                i_ = wq_raw[:, c, q * P:(q + 1) * P].rearrange("p (h m a) -> p a m h", h=HH, a=2)
                dve.mark(VE.tensor_copy(wq_sb[:, c, q, :, :, :], i_))
        dve.mark(VE.tensor_scalar(theta_sb[:, :, :], theta_sb[:, :, :], 1 / (2 * math.pi), None, ALU.mult))
        col = [slope[:, i:i + 1] for i in range(8)]
        need(VE, dve.mark(VE.tensor_scalar(col[1], col[0], -1.0, None, ALU.mult)))
        s = dve.mark(VE.tensor_tensor(col[1], col[0], col[1], ALU.min))
        need(SE, s)
        need(VE, act.mark(SE.activation(col[2], col[1], ACT.Exp)))
        need(VE, dve.mark(VE.tensor_scalar(col[3], col[2], 2.0, None, ALU.add)))
        need(VE, dve.mark(VE.reciprocal(col[3], col[3])))
        need(VE, dve.mark(VE.tensor_tensor(col[3], col[2], col[3], ALU.mult)))
        need(VE, dve.mark(VE.tensor_tensor(col[4], col[3], col[3], ALU.mult)))
        need(VE, dve.mark(VE.memset(col[5], 1.0 / 17)))
        for d in range(15, 0, -2):
            need(VE, dve.mark(VE.tensor_scalar(col[5], col[5], col[4], 1.0 / d, ALU.mult, ALU.add)))
        need(VE, dve.mark(VE.tensor_tensor(col[5], col[5], col[3], ALU.mult)))
        need(VE, dve.mark(VE.tensor_scalar(col[6], col[0], 0.0, None, ALU.max)))
        need(VE, dve.mark(VE.scalar_tensor_tensor(col[7], col[5], 2.0, col[6], ALU.mult, ALU.add)))
        need(VE, dve.mark(VE.tensor_scalar(col[7], col[7], -1.0, None, ALU.mult)))
        need(VE, dists)
        need(VE, dve.mark(VE.tensor_tensor(dist, dist, posn, ALU.add)))
        dve.mark(VE.tensor_scalar(logw_sb[:, :], dist, col[7], None, ALU.mult))
        section_end()

        section(0, False, True)
        with nc.Fori(1, B - 1) as b:
            section(b, True, True)
        section(B - 1, True, False)
        for _ in ffn(x2_dram, out, B - 1):
            pass
        for ln in lines:
            need(SP, (ln, ln.value))


_INS = ["L0_attn_x", "L0_attn_W_mem", "L0_attn_conv_k", "L0_attn_W_q", "L0_attn_theta",
        "L0_attn_decay_slopes", "L0_attn_anchor_slopes", "L0_attn_score_scale", "L0_attn_W_re",
        "L0_attn_W_im", "L0_attn_norm_scale", "L0_attn_W_out", "L0_ffn_gate_w", "L0_ffn_w1",
        "L0_ffn_b1", "L0_ffn_w2", "L0_ffn_b2", "L0_ffn_shared_w1", "L0_ffn_shared_b1",
        "L0_ffn_shared_w2", "L0_ffn_shared_b2"]


def kernel(**inputs):
    import concourse.bacc as bacc
    from concourse.bass_utils import run_bass_kernel_spmd

    nc = bacc.Bacc("TRN2", target_bir_lowering=False, num_devices=1)
    arrays, args = {}, []
    for name in _INS:
        a = np.ascontiguousarray(inputs[name])
        arrays[f"in_{name}"] = a
        args.append(nc.dram_tensor(f"in_{name}", a.shape, mybir.dt.from_np(a.dtype),
                                   kind="ExternalInput").ap())
    args.append(nc.dram_tensor("out_rows", inputs["L0_attn_x"].shape, F32, kind="ExternalOutput").ap())
    macaron(nc, *args)
    r = run_bass_kernel_spmd(nc, [arrays], core_ids=[0])
    return r.results[0]["out_rows"]
```

```python
import math
from contextlib import ExitStack

import numpy as np

import concourse.bass as bass
from concourse import mybir
from concourse.alu_op_type import AluOpType as ALU

F32 = mybir.dt.float32
F32R = mybir.dt.float32r
I32 = mybir.dt.int32
ACT = mybir.ActivationFunctionType
AX = mybir.AxisListType

P = 128
TWO_PI = 6.283185


class Line:

    def __init__(self, sem):
        self.sem, self.value = sem, 0

    def mark(self, instruction, by=1):
        instruction.then_inc(self.sem, by)
        self.value += by
        return (self, self.value)


class Waits:

    def __init__(self):
        self.passed = {}

    def need(self, engine, *points):
        for point in points:
            if point is None:
                continue
            line, value = point
            key = (id(engine), id(line))
            if self.passed.get(key, 0) < value:
                engine.wait_ge(line.sem, value)
                self.passed[key] = value


def macaron(nc, x, w_mem, conv_k, w_q, theta, decay, anchor, score_scale, w_re, w_im, norm_scale,
            w_out, gate_w, w1, b1, w2, b2, sw1, sb1, sw2, sb2, out):
    B, T, D = x.shape
    E, _, H = w1.shape
    SH = sw1.shape[1]
    K, HH, N2 = w_re.shape
    M = theta.shape[4]
    KQ = w_q.shape[1] // (HH * M * 2)
    CW = conv_k.shape[0]
    KH = K * HH
    KC = D // P
    TB = T // P
    HALVES = KH // P
    EC = H // P
    SC = SH // P
    NV = N2 // 2
    VT = K * NV // P
    VH = VT // HALVES
    ND = decay.shape[0]
    KPQ = K // KQ
    KT = P // HH
    QH = KQ // HALVES
    assert (P, T, D) == (128, 512, 512) and HH * M * 2 == P and K == 32 and CW == 4

    ctx = ExitStack()
    with ctx:
        def sb(name, shape, dt=F32):
            return ctx.enter_context(nc.sbuf_tensor(name, shape, dt))

        def line(name):
            return Line(ctx.enter_context(nc.semaphore(name)))

        NW = 2
        w1_ring = sb("w1_ring", [P, NW, 2, KC, H], F32R)
        w2_ring = sb("w2_ring", [P, NW, 2, EC, D], F32R)
        sw1_sb = sb("sw1_sb", [P, 2, KC, SH], F32R)
        sw2_sb = sb("sw2_sb", [P, 2, SC, D], F32R)
        gate_sb = sb("gate_sb", [P, 2, KC, E], F32R)
        gate_raw = sb("gate_raw", [P, KC, E])
        b1_sb = sb("b1_sb", [P, E * EC])
        sb1_sb = sb("sb1_sb", [P, SC])
        wmem_sb = sb("wmem_sb", [P, KC, KH + K])
        wq_sb = sb("wq_sb", [P, KC, KQ, 2, M, HH])
        wbd_sb = sb("wbd_sb", [P, HALVES, 2, 2, KT, NV])
        wout_sb = sb("wout_sb", [P, VT, D])
        conv_sb = sb("conv_sb", [P, HALVES + 1, CW])
        theta_sb = sb("theta_sb", [P, HALVES, M])
        norm_sb = sb("norm_sb", [P, HALVES])
        scale_sb = sb("scale_sb", [K, 1])
        G0 = 2 * K
        low_rows = sb("low_rows", [P, T])
        logw_sb = low_rows[0:K, :]
        b2_sb = low_rows[G0:G0 + E + 1, :]
        ident = sb("ident", [P, P])
        rep_sb = sb("rep_sb", [K, KH])
        before = sb("before", [P, E, E])
        minus_half = sb("minus_half", [P, TB])
        half_pi = sb("half_pi", [P, 1])
        zero1 = sb("zero1", [P, 1])
        slope = sb("slope", [K, 8])

        xin = sb("xin", [P, TB, D])
        stats = sb("stats", [P, TB, 6])
        mv = sb("mv", [P, TB, 2])
        rstd = sb("rstd", [P, 3, TB])
        xnT = sb("xnT", [P, 2, KC, T], F32R)
        NHB = 3
        hT = sb("hT", [P, NHB, T])
        NHP = 2
        hparts = sb("hparts", [P, NHP, 2, T], F32R)
        NGB = 2
        gateT = sb("gateT", [P, NGB, T])
        lg = sb("lg", [P, TB, E])
        cmp_a = sb("cmp_a", [P, TB, E, E])
        cmp_b = sb("cmp_b", [P, TB, E, E])
        rank = sb("rank", [P, TB, E])
        top = sb("top", [P, TB])
        ge = sb("ge", [P, TB, E])
        g9 = sb("g9", [P, TB, E + 1])
        NRES = 4
        res = sb("res", [P, NRES, D])

        kval = sb("kval", [P, HALVES, T])
        pwx = sb("pwx", [P, HALVES, T])
        high_rows = sb("high_rows", [P, 2, T])
        pw = high_rows[0:K, :, :]
        gT = high_rows[G0:G0 + E + 1, 0, :]
        outT = sb("outT", [P, HALVES, 2, T])
        NQX = 2
        qx = sb("qx", [P, NQX, 2, T])
        core = sb("core", [P, 20 * 256])
        turn = core[:, 0:2 * T].rearrange("p (s t) -> p s t", s=2)
        trig = core[:, 2 * T:6 * T].rearrange("p (s c t) -> p s c t", s=2, c=2)
        run = core[:, 6 * T:8 * T].rearrange("p (c t) -> p c t", c=2)
        prod = core[:, 8 * T:10 * T].rearrange("p (c t) -> p c t", c=2)
        anT = core[:, 2 * T:6 * T].rearrange("p (c t) -> p c t", c=KC)
        ZP = T + CW - 1
        zT = core[:, 6 * T:6 * T + 2 * 516].rearrange("p (s t) -> p s t", s=2)
        qT = core[:, 0:2 * T].rearrange("p (s t) -> p s t", s=2)
        yT = core[:, 0:VT * T].rearrange("p (v t) -> p v t", v=VT)
        sil = core[:, VT * T:(VT + 2) * T].rearrange("p (s t) -> p s t", s=2)

        acc = ctx.enter_context(nc.psum_tensor("acc", [P, TB, D], F32))
        hps = ctx.enter_context(nc.psum_tensor("hps", [P, 2, T], F32))
        misc = ctx.enter_context(nc.psum_tensor("misc", [P, 2, T], F32))

        x1_dram = nc.dram_tensor("x1_rows", (B, T, D), F32).ap()
        x2_dram = nc.dram_tensor("x2_rows", (B, T, D), F32).ap()
        q_dram = nc.dram_tensor("q_cols", (KQ, M, HH, 2, T), F32)
        g_dram = nc.dram_tensor("gate_cols", (E + 1, T), F32)
        w1_dram = nc.dram_tensor("w1_parts", (E, P, 2, KC, H), F32).ap()
        w2_dram = nc.dram_tensor("w2_parts", (E, P, 2, EC, D), F32).ap()
        w_dram = (w1_dram, w2_dram)

        pe, act, dve, pool = line("s_pe"), line("s_act"), line("s_dve"), line("s_pool")
        l_xin = line("s_xin")
        l_res = [line(f"s_res{i}") for i in range(NRES)]
        l_gst = line("s_gate_store")
        l_gate = [line(f"s_gate{i}") for i in range(NGB)]
        l_qst = [line(f"s_q_store{i}") for i in range(2)]
        l_qx = [line(f"s_qx{i}") for i in range(NQX)]
        l_const = line("s_const")
        l_shared = line("s_shared_weights")
        l_attn = line("s_attn_weights")
        l_raw = [[line(f"s_raw{i}_{n}") for n in range(NW)] for i in (1, 2)]
        l_w = [[line(f"s_w{i}_{n}") for n in range(NW)] for i in (1, 2)]
        lines = [pe, act, dve, pool, l_xin, *l_res, l_gst, *l_gate, *l_qst, *l_qx, l_const, l_shared,
                 l_attn, *l_raw[0], *l_raw[1], *l_w[0], *l_w[1]]

        PARTS = ((0, 0), (0, 1), (1, 0))
        PE, VE, SE, GE, SP = nc.tensor, nc.vector, nc.scalar, nc.gpsimd, nc.sync
        waits = Waits()
        need = waits.need
        free = {}
        turns = {}

        def take(name, n):
            i = turns.get(name, 0)
            turns[name] = i + 1
            return i % n

        def section_end():
            for ln in lines:
                need(SP, (ln, ln.value))
            nc.all_engine_barrier()
            nums = [ln.sem for ln in lines]
            for s in nums:
                GE.sem_clear(s)
            nc.all_engine_barrier()
            for ln in lines:
                ln.value = 0
            waits.passed.clear()
            free.clear()
            turns.clear()

        def rows(dram, b):
            return bass.AP(dram.tensor, dram.offset + b * (T * D), [[D, P], [P * D, TB], [1, D]])

        def row_tile(dram, b, tb):
            return bass.AP(dram.tensor, dram.offset + b * (T * D) + tb * P * D, [[D, P], [1, D]])

        def normalise(src, b):
            need(SP, free.get("xin"))
            loaded = l_xin.mark(SP.dma_start(xin[:, :, :], rows(src, b)), 16)
            need(VE, loaded)
            for tb in range(TB):
                s = dve.mark(VE.bn_stats(stats[:, tb, :], xin[:, tb, :]))
            need(VE, s)
            for tb in range(TB):
                s = dve.mark(VE.bn_aggr(mv[:, tb, :], stats[:, tb, :]))
            need(GE, s)
            r, v, u = rstd[:, 0, :], rstd[:, 1, :], rstd[:, 2, :]
            need(GE, pool.mark(GE.tensor_scalar(v, mv[:, :, 1], 1e-5, None, ALU.add)))
            need(GE, pool.mark(GE.tensor_tensor(r, v, minus_half[:, :], ALU.pow)))
            need(GE, pool.mark(GE.tensor_tensor(u, r, r, ALU.mult)))
            need(GE, pool.mark(GE.tensor_tensor(u, u, v, ALU.mult)))
            need(GE, pool.mark(GE.tensor_scalar(u, u, -0.5, 1.5, ALU.mult, ALU.add)))
            rstd_ready = pool.mark(GE.tensor_tensor(r, r, u, ALU.mult))

            def finish():
                need(VE, rstd_ready)
                return [dve.mark(VE.tensor_scalar(xin[:, tb, :], xin[:, tb, :], mv[:, tb, 0:1],
                                                  rstd[:, 0, tb:tb + 1], ALU.subtract, ALU.mult))
                        for tb in range(TB)]
            return finish

        def turn_tile(tb, ready):
            bank = take("misc", 2)
            need(PE, ready, free.get(("misc", bank)))
            for c in range(KC):
                t = PE.transpose(misc[:, bank, c * P:(c + 1) * P], xin[:, tb, c * P:(c + 1) * P],
                                 ident[:, :])
            free["xin"] = pe.mark(t)
            return bank, free["xin"], misc[:, bank, :].rearrange("p (c t) -> p c t", c=KC)

        def turn_into(dst, tb, normalised):
            bank, turned, cols = turn_tile(tb, normalised[tb])
            need(SE, turned)
            free["misc", bank] = act.mark(SE.copy(dst[:, :, tb * P:(tb + 1) * P], cols))
            return free["misc", bank]

        def turn_into_parts(dst, tb, normalised):
            need(SE, free.get("xnT"))
            need(VE, free.get("xnT"))
            bank, turned, cols = turn_tile(tb, normalised[tb])
            high, low = (dst[:, i, :, tb * P:(tb + 1) * P] for i in range(2))
            need(SE, turned)
            need(VE, act.mark(SE.copy(high, cols)))
            free["misc", bank] = dve.mark(VE.tensor_tensor(low, cols, high.bitcast(F32),
                                                           ALU.subtract))
            return free["misc", bank]

        def gates(xn_ready, result):
            bank = take("misc", 2)
            need(PE, xn_ready, free.get(("misc", bank)))
            for tb in range(TB):
                for c in range(KC):
                    for i, (xp, wp) in enumerate(PARTS):
                        t = PE.matmul(misc[:, bank, tb * E:(tb + 1) * E],
                                      xnT[:, xp, c, tb * P:(tb + 1) * P], gate_sb[:, wp, c, :],
                                      start=c == 0 and i == 0, stop=c == KC - 1 and i == 2)
            need(VE, pe.mark(t))
            s = dve.mark(VE.tensor_copy(lg[:, :, :],
                                        misc[:, bank, 0:TB * E].rearrange("p (t e) -> p t e", e=E)))
            free["misc", bank] = s
            need(VE, s)
            other = lg[:, :, None, :].broadcast_to([P, TB, E, E])
            own = lg[:, :, :, None].broadcast_to([P, TB, E, E])
            low = before[:, None, :, :].broadcast_to([P, TB, E, E])
            dve.mark(VE.tensor_tensor(cmp_a[:, :, :, :], other, own, ALU.is_gt))
            dve.mark(VE.tensor_reduce(top[:, :], lg[:, :, :], AX.X, ALU.max))
            need(VE, dve.mark(VE.tensor_tensor(cmp_b[:, :, :, :], other, own, ALU.is_equal)))
            need(VE, dve.mark(VE.tensor_tensor(cmp_b[:, :, :, :], cmp_b[:, :, :, :], low, ALU.mult)))
            s = dve.mark(VE.tensor_tensor(ge[:, :, :], lg[:, :, :],
                                          top[:, :, None].broadcast_to([P, TB, E]), ALU.subtract))
            yield
            need(SE, s)
            e = act.mark(SE.activation(ge[:, :, :], ge[:, :, :], ACT.Exp))
            need(VE, dve.mark(VE.tensor_tensor(cmp_a[:, :, :, :], cmp_a[:, :, :, :],
                                               cmp_b[:, :, :, :], ALU.add)))
            need(VE, dve.mark(VE.tensor_reduce(rank[:, :, :], cmp_a[:, :, :, :], AX.X, ALU.add)))
            need(VE, dve.mark(VE.tensor_scalar(rank[:, :, :], rank[:, :, :], 1.5, None, ALU.is_lt)))
            need(VE, e)
            need(VE, dve.mark(VE.tensor_tensor(ge[:, :, :], ge[:, :, :], rank[:, :, :], ALU.mult)))
            need(VE, dve.mark(VE.tensor_reduce(top[:, :], ge[:, :, :], AX.X, ALU.add)))
            need(VE, dve.mark(VE.reciprocal(top[:, :], top[:, :])))
            s = dve.mark(VE.tensor_tensor(g9[:, :, 0:E], ge[:, :, :],
                                          top[:, :, None].broadcast_to([P, TB, E]), ALU.mult))
            yield
            bank = take("misc", 2)
            need(PE, s, free.get(("misc", bank)))
            for tb in range(TB):
                t = PE.transpose(misc[0:E + 1, bank, tb * P:(tb + 1) * P], g9[:, tb, :], ident[:, :])
            t = pe.mark(t)
            need(VE, t, free.get("gT"))
            gT_ready = dve.mark(VE.tensor_copy(gT[:, :], misc[0:E + 1, bank, :]))
            free["misc", bank] = gT_ready
            need(SP, gT_ready, free.get("g_dram"))
            stored = l_gst.mark(SP.dma_start(g_dram.ap(), gT[:, :]), 16)
            result["gT"], result["stored"] = gT_ready, stored
            yield

        def ring(i, slot):
            return (w1_ring if i == 0 else w2_ring)[:, slot, :, :, :]

        def raw_weights(e, i):
            slot = e % NW
            raw = raw_w(slot)[i]
            src = (w1 if i == 0 else w2)[e].rearrange("(c p) n -> p c n", p=P)
            need(SP, free.get(("raw", i, slot)))
            there = l_raw[i][slot].mark(SP.dma_start(raw, src), 16)
            high, low = ring(i, slot)[:, 0, :, :], ring(i, slot)[:, 1, :, :]
            stored = (l_w[i][slot], l_w[i][slot].value)
            need(SE, there, free.get(("w", i, slot)), stored)
            need(VE, there, free.get(("w", i, slot)), stored)
            need(VE, act.mark(SE.copy(high, raw)))
            done = dve.mark(VE.tensor_tensor(low, raw, high.bitcast(F32), ALU.subtract))
            free["raw", i, slot] = done
            need(SP, done)
            l_w[i][slot].mark(SP.dma_start(w_dram[i][e], ring(i, slot).bitcast(F32)), 16)
            return done

        def load_weights(e, i):
            slot = e % NW
            need(SP, free.get(("w", i, slot)))
            return l_w[i][slot].mark(SP.dma_start(ring(i, slot).bitcast(F32), w_dram[i][e]), 16)

        TILES = [("shared", j) for j in range(SC)] + [("routed", j) for j in range(E * EC)]
        NT = len(TILES)
        LAG = 3
        GATE_WORK = 3

        def ffn(jobs):
            hidden = {}
            state = [{} for _ in jobs]
            total = NT * len(jobs)

            def gate(k):
                q, n = divmod(k, NT)
                kind, j = TILES[n]
                if kind == "shared":
                    return
                e = j // EC
                slot, ready = hidden[k]
                g, gate_there = state[q]["gate"][e]
                need(VE, ready, gate_there)
                ready = dve.mark(VE.tensor_tensor(hT[:, slot, :], hT[:, slot, :], gateT[:, g, :],
                                                  ALU.mult))
                free["gateT", g] = ready
                hidden[k] = (slot, ready)

            def parts(k):
                slot, ready = hidden[k]
                p = k % NHP
                high, low = hparts[:, p, 0, :], hparts[:, p, 1, :]
                need(SE, ready, free.get(("hparts", p)))
                need(VE, act.mark(SE.copy(high, hT[:, slot, :])), free.get(("hparts", p)))
                s = dve.mark(VE.tensor_tensor(low, hT[:, slot, :], high.bitcast(F32), ALU.subtract))
                free["hT", slot] = s
                hidden[k] = s

            def follow(q, e, i, used):
                free["w", i, e % NW] = used
                if e + NW < E:
                    state[q]["w", e + NW, i] = jobs[q][3](e + NW, i)
                elif q + 1 < len(jobs):
                    state[q + 1]["w", e + NW - E, i] = jobs[q + 1][3](e + NW - E, i)

            def accumulate(k):
                q, n = divmod(k, NT)
                kind, j = TILES[n]
                src, dst, b, provide = jobs[q]
                p = k % NHP
                if n == 0:
                    state[q]["res"] = {}
                if n == SC:
                    need(PE, state[q]["gT"])
                    for tb in range(TB):
                        t = PE.matmul(acc[:, tb, :], gT[:, tb * P:(tb + 1) * P], b2_sb,
                                      start=False, stop=False)
                    free["gT"] = pe.mark(t)
                need(PE, hidden.pop(k))
                if kind == "routed":
                    need(PE, state[q]["w", j // EC, 1])
                for tb in range(TB):
                    if n == 0:
                        need(PE, free.get(("acc", tb)))
                    for i, (hp, wp) in enumerate(PARTS):
                        w = sw2_sb[:, wp, j, :] if kind == "shared" else \
                            w2_ring[:, (j // EC) % NW, wp, j % EC, :]
                        t = PE.matmul(acc[:, tb, :], hparts[:, p, hp, tb * P:(tb + 1) * P], w,
                                      start=n == 0 and i == 0, stop=n == NT - 1 and i == 2)
                done = pe.mark(t)
                free["hparts", p] = done
                if kind == "routed" and j % EC == EC - 1:
                    follow(q, j // EC, 1, done)
                if n == NT - 2:
                    state[q]["res"] = {tb: load_rows(src, b, tb) for tb in range(TB)}
                if n == NT - 1:
                    for tb in range(TB):
                        free["acc", tb] = store_rows(state[q]["res"][tb], dst, b, tb, acc[:, tb, :],
                                                     done, 0.5)

            for e in range(NW):
                for i in range(2):
                    state[0]["w", e, i] = jobs[0][3](e, i)
            state[0]["finish"] = normalise(jobs[0][0], jobs[0][2])
            yield 0.0
            for k in range(total + LAG):
                q, n = divmod(k, NT)
                if k < total:
                    st = state[q]
                    if n == 0:
                        normalised = st["finish"]()
                        xn_ready = [turn_into_parts(xnT, tb, normalised) for tb in range(2)]
                        if k >= 1:
                            gate(k - 1)
                            parts(k - 2)
                            accumulate(k - LAG)
                        xn_ready += [turn_into_parts(xnT, tb, normalised) for tb in range(2, TB)]
                        st["xn"] = xn_ready[-1]
                        st["gates"] = gates(st["xn"], st)
                        st["gate"] = {}
                    kind, j = TILES[n]
                    e = j // EC
                    if kind == "routed" and j % EC == 0:
                        g = take("gateT", NGB)
                        need(SP, st["stored"], free.get(("gateT", g)))
                        st["gate"][e] = (g, l_gate[g].mark(
                            SP.dma_start(gateT[:, g, :], bass.AP(g_dram, e * T, [[0, P], [1, T]])), 16))
                        free["g_dram"] = st["gate"][e][1]
                    bank = take("hps", 2)
                    need(PE, st["xn"], free.get(("hps", bank)))
                    if kind == "routed":
                        need(PE, st["w", e, 0])
                    for c in range(KC):
                        for i, (wp, xp) in enumerate(PARTS):
                            w = sw1_sb[:, wp, c, j * P:(j + 1) * P] if kind == "shared" else \
                                w1_ring[:, e % NW, wp, c, (j % EC) * P:(j % EC + 1) * P]
                            t = PE.matmul(hps[:, bank, :], w, xnT[:, xp, c, :],
                                          start=c == 0 and i == 0, stop=c == KC - 1 and i == 2)
                    made = pe.mark(t)
                    free["xnT"] = made
                    if kind == "routed" and j % EC == EC - 1:
                        follow(q, e, 0, made)
                yield 2.55
                late = n == 0 and 0 < k < total
                if not late:
                    if 0 <= k - 1 < total:
                        gate(k - 1)
                    if 0 <= k - 2 < total:
                        parts(k - 2)
                if k < total:
                    slot = take("hT", NHB)
                    need(SE, made, free.get(("hT", slot)))
                    bias = sb1_sb[:, j:j + 1] if kind == "shared" else b1_sb[:, j:j + 1]
                    ready = act.mark(SE.activation(hT[:, slot, :], hps[:, bank, :], ACT.Gelu,
                                                   bias=bias))
                    free["hps", bank] = ready
                    hidden[k] = (slot, ready)
                if k >= LAG and not late:
                    accumulate(k - LAG)
                if k < total and n < GATE_WORK:
                    next(st["gates"])
                if k < total and n == NT // 2 and q + 1 < len(jobs):
                    state[q + 1]["finish"] = normalise(jobs[q + 1][0], jobs[q + 1][2])
                yield 2.55

        def load_rows(src, b, tb):
            s = take("res", NRES)
            need(SP, free.get(("res", s)))
            return s, l_res[s].mark(SP.dma_start(res[:, s, :], row_tile(src, b, tb)), 16)

        def store_rows(slot_loaded, dst, b, tb, result, ready, factor):
            s, loaded = slot_loaded
            need(VE, ready, loaded)
            summed = dve.mark(VE.scalar_tensor_tensor(res[:, s, :], result, factor, res[:, s, :],
                                                      ALU.mult, ALU.add))
            need(SP, summed)
            free["res", s] = l_res[s].mark(SP.dma_start(row_tile(dst, b, tb), res[:, s, :]), 16)
            return summed

        def spread(half, i, *ready):
            bank = take("misc", 2)
            need(PE, *ready, free.get(("misc", bank)))
            return bank, pe.mark(PE.matmul(misc[:, bank, :], rep_sb[:, half * P:(half + 1) * P],
                                           pw[:, i, :], start=True, stop=True))

        def attention_inputs(b, an_ready):
            need(PE, (l_attn, l_attn.value))
            conv_done = {}
            for i in range(HALVES + 1):
                rowsn = P if i < HALVES else K
                bank = take("misc", 2)
                need(PE, an_ready, free.get(("misc", bank)))
                for c in range(KC):
                    t = PE.matmul(misc[0:rowsn, bank, :], wmem_sb[:, c, i * P:i * P + rowsn],
                                  anT[:, c, :], start=c == 0, stop=c == KC - 1)
                z = zT[0:rowsn, i % 2, :]
                need(SE, pe.mark(t), conv_done.get(i - 2))
                if i < 2:
                    need(VE, dve.mark(VE.memset(z[:, 0:CW - 1], 0.0)))
                s = act.mark(SE.copy(z[:, CW - 1:ZP], misc[0:rowsn, bank, :]))
                free["misc", bank] = s
                need(VE, s)
                o = kval[:, i, :] if i < HALVES else pw[:, 0, :]
                s = dve.mark(VE.tensor_scalar(o, z[:, 0:T], conv_sb[0:rowsn, i, 0:1], None, ALU.mult))
                for k in range(1, CW):
                    need(VE, s)
                    s = dve.mark(VE.scalar_tensor_tensor(o, z[:, k:k + T],
                                                         conv_sb[0:rowsn, i, k:k + 1], o,
                                                         ALU.mult, ALU.add))
                conv_done[i] = s
                yield 3.4
            need(VE, s)
            p, den = pw[:, 0, :], pw[:, 1, :]
            need(VE, dve.mark(VE.tensor_scalar(p, p, scale_sb[:, 0:1], 20.0, ALU.mult, ALU.min)))
            s = dve.mark(VE.scalar_tensor_tensor(p, p, -20.0, logw_sb[:, :], ALU.max, ALU.add))
            need(SE, s)
            s = act.mark(SE.activation(p, p, ACT.Exp))
            need(VE, s)
            need(VE, dve.mark(VE.tensor_tensor_scan(den, p, zero1[0:K, 0:1].broadcast_to([K, T]), 0.0,
                                                    ALU.add, ALU.add)))
            need(VE, dve.mark(VE.tensor_scalar(den, den, 1e-4, None, ALU.max)))
            den_ready = dve.mark(VE.reciprocal(den, den))
            for q in range(KQ):
                bank = take("misc", 2)
                need(PE, free.get(("misc", bank)))
                for c in range(KC):
                    t = PE.matmul(misc[:, bank, :], wq_sb[:, c, q, :, :, :].rearrange("p a b c -> p (a b c)"),
                                  anT[:, c, :], start=c == 0, stop=c == KC - 1)
                t = pe.mark(t)
                free["anT"] = t
                need(SE, t, free.get(("qT", q % 2)))
                s = act.mark(SE.copy(qT[:, q % 2, :], misc[:, bank, :]))
                free["misc", bank] = s
                need(SP, s)
                free["qT", q % 2] = l_qst[q % 2].mark(
                    SP.dma_start(bass.AP(q_dram, q * P * T, [[T, 2], [2 * T, M * HH], [1, T]]), qT[:, q % 2, :]), 16)
                yield 3.4
            for half in range(HALVES):
                bank, t = spread(half, 0, den_ready)
                need(SE, t)
                free["misc", bank] = act.mark(SE.copy(pwx[:, half, :], misc[:, bank, :]))
            free["spread"] = free["misc", bank]
            yield 1.0

        def attention_core(b):
            steps = [(half, m) for half in range(HALVES) for m in range(M)]
            front = {}

            def load_queries(n):
                half, m = steps[n]
                s = n % NQX
                need(SP, free.get(("qx", s)), *[(ln, ln.value) for ln in l_qst])
                for g in range(QH):
                    q = half * QH + g
                    src = bass.AP(q_dram, q * P * T + m * HH * 2 * T,
                                  [[0, KPQ], [2 * T, HH], [1, 2 * T]])
                    at = l_qx[s].mark(SP.dma_start(qx[g * KPQ * HH:(g + 1) * KPQ * HH, s, :, :], src), 16)
                front[n, "q"] = at

            def phases(n):
                half, m = steps[n]
                s = n % 2
                f, nearest = turn[:, s, :], prod_int(s)
                th = theta_sb[:, half, m:m + 1]
                need(VE, free.get(("turn", s)), *[(ln, ln.value) for ln in l_qst])
                r = dve.mark(VE.tensor_scalar(nearest, kval[:, half, :], th, None, ALU.mult))
                need(VE, r)
                r = dve.mark(VE.scalar_tensor_tensor(f, kval[:, half, :], th, nearest,
                                                     ALU.mult, ALU.subtract))
                need(SE, r, free.get(("trig", s)), free.get("anT"))
                a = act.mark(SE.activation(trig[:, s, 0, :], f, ACT.Abs))
                act.mark(SE.activation(trig[:, s, 1, :], f, ACT.Sin, scale=TWO_PI))
                need(SE, a)
                a = act.mark(SE.activation(trig[:, s, 0, :], trig[:, s, 0, :], ACT.Sin,
                                           scale=-TWO_PI, bias=half_pi[:, 0:1]))
                free["turn", s] = a
                front[n] = a

            def prod_int(s):
                return turn[:, s, :].bitcast(I32)

            def sums(n):
                half, m = steps[n]
                s, qs = n % 2, n % NQX
                cs = trig[:, s, :, :]
                need(VE, front[n], free["spread"])
                w = dve.mark(VE.tensor_tensor(cs, cs, pwx[:, half, None, :].broadcast_to([P, 2, T]),
                                              ALU.mult))
                yield 1.6
                need(VE, w)
                for c in range(2):
                    w = dve.mark(VE.tensor_tensor_scan(run[:, c, :], trig[:, s, c, :],
                                                       zero1[:, 0:1].broadcast_to([P, T]), 0.0,
                                                       ALU.add, ALU.add))
                free["trig", s] = w
                yield 1.6
                need(VE, w, front[n, "q"])
                w = dve.mark(VE.tensor_tensor(prod[:, :, :], run[:, :, :], qx[:, qs, :, :], ALU.mult))
                yield 1.6
                need(VE, w)
                back = bass.AP(run.tensor, run.offset + T, [list(run.ap[0]), [-T, 2], [1, T]])
                w3 = dve.mark(VE.tensor_tensor(qx[:, qs, :, :], back, qx[:, qs, :, :], ALU.mult))
                yield 1.6
                re, im = outT[:, half, 0, :], outT[:, half, 1, :]
                if m == 0:
                    dve.mark(VE.tensor_tensor(re, prod[:, 0, :], prod[:, 1, :], ALU.add))
                    need(VE, w3)
                    w3 = dve.mark(VE.tensor_tensor(im, qx[:, qs, 0, :], qx[:, qs, 1, :], ALU.subtract))
                else:
                    w = dve.mark(VE.tensor_tensor(prod[:, 0, :], prod[:, 0, :], prod[:, 1, :], ALU.add))
                    need(VE, w3)
                    w3 = dve.mark(VE.tensor_tensor(qx[:, qs, 0, :], qx[:, qs, 0, :], qx[:, qs, 1, :],
                                                   ALU.subtract))
                    yield 1.6
                    need(VE, w)
                    dve.mark(VE.tensor_tensor(re, re, prod[:, 0, :], ALU.add))
                    need(VE, w3)
                    w3 = dve.mark(VE.tensor_tensor(im, im, qx[:, qs, 0, :], ALU.add))
                free["qx", qs] = w3
                yield 1.6
                if m == M - 1:
                    bank, t = spread(half, 1)
                    need(VE, t, w3)
                    for part in range(2):
                        o = outT[:, half, part, :]
                        w3 = dve.mark(VE.scalar_tensor_tensor(o, o, norm_sb[:, half:half + 1],
                                                              misc[:, bank, :], ALU.mult, ALU.mult))
                    free["misc", bank] = w3
                    free["outT", half] = w3
                    yield 1.8

            load_queries(0)
            phases(0)
            yield 0.0
            for n in range(len(steps)):
                if n + 1 < len(steps):
                    load_queries(n + 1)
                    phases(n + 1)
                yield 1.6
                yield from sums(n)

        def attention_output(b):
            yT_ready = []
            core_done = free["outT", HALVES - 1]
            psum = {"misc": misc, "hps": hps}
            for v in range(VT):
                half, j = v // VH, v % VH
                banks = []
                for vg, pair in enumerate(("misc", "hps")):
                    bank = take(pair, 2)
                    banks.append(bank)
                    need(PE, free["outT", half], free.get((pair, bank)))
                    for part in range(2):
                        w = wbd_sb[:, half, part, vg, :, :].rearrange("p k n -> p (k n)")
                        t = PE.matmul(psum[pair][:, bank, :], w[:, j * P:(j + 1) * P],
                                      outT[:, half, part, :], start=part == 0, stop=part == 1)
                    t = pe.mark(t)
                need(SE, t, core_done, free.get(("sil", v % 2)))
                s = act.mark(SE.activation(sil[:, v % 2, :], hps[:, banks[1], :], ACT.Silu))
                free["hps", banks[1]] = s
                yield 1.7
                need(VE, s)
                s = dve.mark(VE.tensor_tensor(yT[:, v, :], misc[:, banks[0], :], sil[:, v % 2, :],
                                              ALU.mult))
                free["misc", banks[0]] = s
                free["sil", v % 2] = s
                yield 1.7
            loaded = [load_rows(x1_dram, b, tb) for tb in range(TB)]
            for tb in range(TB):
                bank = take("misc", 2)
                need(PE, s, free.get(("misc", bank)))
                for v in range(VT):
                    t = PE.matmul(misc[:, bank, :], yT[:, v, tb * P:(tb + 1) * P], wout_sb[:, v, :],
                                  start=v == 0, stop=v == VT - 1)
                t = pe.mark(t)
                yield 5.1
                free["misc", bank] = store_rows(loaded[tb], x2_dram, b, tb, misc[:, bank, :],
                                                t, 1.0)

        def chain(*parts):
            for p in parts:
                yield from p

        def together(a, f):
            ta = tf = 0.0
            live = [a, f]
            while live:
                g = live[0] if len(live) == 1 else (a if ta <= tf else f)
                try:
                    c = next(g)
                except StopIteration:
                    live.remove(g)
                    continue
                if g is a:
                    ta += c
                else:
                    tf += c

        def section(b, second_ffn, first_ffn):
            jobs = []
            if second_ffn:
                jobs.append((x2_dram, out, b - 1, load_weights))
            if first_ffn:
                jobs.append((x, x1_dram, b + 1, load_weights))
            normalised = normalise(x1_dram, b)()
            for tb in range(TB):
                an_ready = turn_into(anT, tb, normalised)
            together(chain(attention_inputs(b, an_ready), attention_core(b), attention_output(b)), ffn(jobs))
            section_end()

        def load(ln, dst, src, eng=SP):
            return ln.mark(eng.dma_start(dst, src), 16)

        nc_dma = nc.allow_non_contiguous_dma(reason="small bias and scale vectors, loaded once")
        ctx.enter_context(nc_dma)
        core_raw = core[:, 0:4096].rearrange("p (i n) -> p i n", i=2)

        def raw_w(slot):
            r = core_raw[:, slot, :].rearrange("p (i n) -> p i n", i=2)
            return (r[:, 0, :].rearrange("p (c h) -> p c h", c=KC),
                    r[:, 1, :].rearrange("p (c d) -> p c d", c=EC))

        load(l_const, gate_raw[:, :, :], gate_w.rearrange("(c p) e -> p c e", p=P), SE)
        load(l_shared, core_raw[:, 0, :].rearrange("p (c h) -> p c h", c=KC),
             sw1.rearrange("(c p) h -> p c h", p=P), SE)
        load(l_shared, core_raw[:, 1, :].rearrange("p (c d) -> p c d", c=SC),
             sw2.rearrange("(c p) d -> p c d", p=P), SE)
        load(l_const, sb1_sb[:, :], sb1.rearrange("(c p) -> p c", p=P), SE)
        load(l_const, b1_sb[:, :], b1.rearrange("e (c p) -> p (e c)", p=P), SE)
        load(l_const, b2_sb[0:E, :], b2, SE)
        load(l_const, b2_sb[E:E + 1, :], sb2.rearrange("(a d) -> a d", a=1), SE)
        load(l_attn, theta_sb[:, :, :], theta.rearrange("a b (g k) h m -> (a b k h) g m", g=HALVES), SE)
        load(l_attn, norm_sb[:, :], norm_scale.rearrange("a b (g k) h -> (a b k h) g", g=HALVES), SE)
        for i in range(HALVES + 1):
            rowsn = P if i < HALVES else K
            load(l_attn, conv_sb[0:rowsn, i, :],
                 conv_k[:, 0, i * P:i * P + rowsn].rearrange("w p -> p w"), SE)
        load(l_attn, scale_sb[:, :], score_scale.rearrange("(p a) -> p a", a=1), SE)
        load(l_attn, slope[0:ND, 0:1], decay.rearrange("(p a) -> p a", a=1), SE)
        load(l_attn, slope[ND:K, 0:1], anchor.rearrange("(p a) -> p a", a=1), SE)
        load(l_attn, wmem_sb[:, :, :], w_mem.rearrange("(c p) n -> p c n", p=P), SE)
        load(l_attn, wout_sb[:, :, :], w_out.rearrange("(v p) d -> p v d", p=P), SE)

        def pg(i):
            return pool.mark(i)

        pg(GE.memset(minus_half[:, :], -0.5))
        pg(GE.memset(half_pi[:, :], math.pi / 2))
        pg(GE.memset(zero1[:, :], 0.0))
        pg(GE.memset(g9[:, :, :], 1.0))
        pg(GE.memset(before[:, :, :], 1.0))
        pg(GE.memset(rep_sb[:, :], 1.0))
        need(GE, pg(GE.memset(ident[:, :], 0.0)))
        ident_ready = pg(GE.affine_select(out=ident[:, :], in_=ident[:, :], compare_op=ALU.not_equal,
                                          fill=1.0, base=0, pattern=[[-1, P]], channel_multiplier=1))
        pg(GE.affine_select(out=before[:, :, :], in_=before[:, :, :], compare_op=ALU.is_gt, fill=0.0,
                            base=0, pattern=[[1, E], [-1, E]], channel_multiplier=0))
        need(GE, pg(GE.affine_select(out=rep_sb[:, :], in_=rep_sb[:, :], compare_op=ALU.is_ge, fill=0.0,
                                     base=0, pattern=[[1, KH]], channel_multiplier=-HH)))
        consts = pg(GE.affine_select(out=rep_sb[:, :], in_=rep_sb[:, :], compare_op=ALU.is_ge, fill=0.0,
                                     base=HH - 1, pattern=[[-1, KH]], channel_multiplier=HH))

        need(PE, consts)
        need(VE, consts)
        need(SE, consts)
        for eng in (PE, SE, VE):
            need(eng, (l_const, l_const.value))
        for raw, dst in ((gate_raw[:, :, :], gate_sb),
                         (core_raw[:, 0, :].rearrange("p (c h) -> p c h", c=KC), sw1_sb),
                         (core_raw[:, 1, :].rearrange("p (c d) -> p c d", c=SC), sw2_sb)):
            if dst is sw1_sb:
                need(SE, (l_shared, l_shared.value))
                need(VE, (l_shared, l_shared.value))
            need(VE, act.mark(SE.copy(dst[:, 0, :, :], raw)))
            s = dve.mark(VE.tensor_tensor(dst[:, 1, :, :], raw, dst[:, 0, :, :].bitcast(F32),
                                          ALU.subtract))
        for slot in range(NW):
            free["raw", 0, slot] = free["raw", 1, slot] = s
        need(PE, s)
        for _ in ffn([(x, x1_dram, 0, raw_weights)]):
            pass

        need(SP, *[free["raw", i, slot] for i in range(2) for slot in range(NW)])
        wq_raw = core[:, 2 * T:2 * T + KC * KQ * P].rearrange("p (c n) -> p c n", c=KC)
        load(l_attn, wq_raw, w_q.rearrange("(c p) n -> p c n", p=P))
        w_raw = core[:, 0:2 * HALVES * N2].rearrange("p (i g n) -> p i g n", i=2, g=HALVES)
        load(l_attn, w_raw[:, 0, :, :], w_re.rearrange("(g k) h n -> (k h) g n", g=HALVES))
        load(l_attn, w_raw[:, 1, :, :], w_im.rearrange("(g k) h n -> (k h) g n", g=HALVES))
        dist, posn = hT[0:K, 0, :], hT[0:K, 1, :]
        need(GE, (pe, pe.value))
        pg(GE.iota(dist, pattern=[[-1, T]], base=T - 1, channel_multiplier=0,
                   allow_small_or_imprecise_dtypes=True))
        need(GE, pg(GE.iota(posn, pattern=[[1, T]], base=0, channel_multiplier=0,
                            allow_small_or_imprecise_dtypes=True)))
        pg(GE.affine_select(out=dist, in_=dist, compare_op=ALU.is_gt, fill=0.0, base=ND,
                            pattern=[[0, T]], channel_multiplier=-1))
        dists = pg(GE.affine_select(out=posn, in_=posn, compare_op=ALU.is_ge, fill=0.0, base=-ND,
                                    pattern=[[0, T]], channel_multiplier=1))
        need(GE, (l_attn, l_attn.value))
        for half in range(HALVES):
            for part in range(2):
                for vg in range(2):
                    o = wbd_sb[:, half, part, vg, :, :]
                    i_ = w_raw[:, part, half, None, vg * NV:(vg + 1) * NV].broadcast_to([P, KT, NV])
                    need(GE, pg(GE.affine_select(out=o, in_=i_, compare_op=ALU.is_ge, fill=0.0, base=0,
                                                 pattern=[[-HH, KT], [0, NV]], channel_multiplier=1)))
                    wbd_ready = pg(GE.affine_select(out=o, in_=o, compare_op=ALU.is_ge, fill=0.0,
                                                    base=HH - 1, pattern=[[HH, KT], [0, NV]],
                                                    channel_multiplier=-1))
        need(VE, (l_attn, l_attn.value))
        for c in range(KC):
            for q in range(KQ):
                i_ = wq_raw[:, c, q * P:(q + 1) * P].rearrange("p (h m a) -> p a m h", h=HH, a=2)
                dve.mark(VE.tensor_copy(wq_sb[:, c, q, :, :, :], i_))
        dve.mark(VE.tensor_scalar(theta_sb[:, :, :], theta_sb[:, :, :], 1 / (2 * math.pi), None, ALU.mult))
        col = [slope[:, i:i + 1] for i in range(8)]
        need(VE, dve.mark(VE.tensor_scalar(col[1], col[0], -1.0, None, ALU.mult)))
        s = dve.mark(VE.tensor_tensor(col[1], col[0], col[1], ALU.min))
        need(SE, s)
        need(VE, act.mark(SE.activation(col[2], col[1], ACT.Exp)))
        need(VE, dve.mark(VE.tensor_scalar(col[3], col[2], 2.0, None, ALU.add)))
        need(VE, dve.mark(VE.reciprocal(col[3], col[3])))
        need(VE, dve.mark(VE.tensor_tensor(col[3], col[2], col[3], ALU.mult)))
        need(VE, dve.mark(VE.tensor_tensor(col[4], col[3], col[3], ALU.mult)))
        need(VE, dve.mark(VE.memset(col[5], 1.0 / 17)))
        for d in range(15, 0, -2):
            need(VE, dve.mark(VE.tensor_scalar(col[5], col[5], col[4], 1.0 / d, ALU.mult, ALU.add)))
        need(VE, dve.mark(VE.tensor_tensor(col[5], col[5], col[3], ALU.mult)))
        need(VE, dve.mark(VE.tensor_scalar(col[6], col[0], 0.0, None, ALU.max)))
        need(VE, dve.mark(VE.scalar_tensor_tensor(col[7], col[5], 2.0, col[6], ALU.mult, ALU.add)))
        need(VE, dve.mark(VE.tensor_scalar(col[7], col[7], -1.0, None, ALU.mult)))
        need(VE, dists)
        need(VE, dve.mark(VE.tensor_tensor(dist, dist, posn, ALU.add)))
        dve.mark(VE.tensor_scalar(logw_sb[:, :], dist, col[7], None, ALU.mult))
        section_end()

        section(0, False, True)
        with nc.Fori(1, B - 1) as b:
            section(b, True, True)
        section(B - 1, True, False)
        for _ in ffn([(x2_dram, out, B - 1, load_weights)]):
            pass
        for ln in lines:
            need(SP, (ln, ln.value))


_INS = ["L0_attn_x", "L0_attn_W_mem", "L0_attn_conv_k", "L0_attn_W_q", "L0_attn_theta",
        "L0_attn_decay_slopes", "L0_attn_anchor_slopes", "L0_attn_score_scale", "L0_attn_W_re",
        "L0_attn_W_im", "L0_attn_norm_scale", "L0_attn_W_out", "L0_ffn_gate_w", "L0_ffn_w1",
        "L0_ffn_b1", "L0_ffn_w2", "L0_ffn_b2", "L0_ffn_shared_w1", "L0_ffn_shared_b1",
        "L0_ffn_shared_w2", "L0_ffn_shared_b2"]


def kernel(**inputs):
    import concourse.bacc as bacc
    from concourse.bass_utils import run_bass_kernel_spmd

    nc = bacc.Bacc("TRN2", target_bir_lowering=False, num_devices=1)
    arrays, args = {}, []
    for name in _INS:
        a = np.ascontiguousarray(inputs[name])
        arrays[f"in_{name}"] = a
        args.append(nc.dram_tensor(f"in_{name}", a.shape, mybir.dt.from_np(a.dtype),
                                   kind="ExternalInput").ap())
    args.append(nc.dram_tensor("out_rows", inputs["L0_attn_x"].shape, F32, kind="ExternalOutput").ap())
    macaron(nc, *args)
    r = run_bass_kernel_spmd(nc, [arrays], core_ids=[0])
    return r.results[0]["out_rows"]
```

```python
import math
from contextlib import ExitStack

import numpy as np

import concourse.bass as bass
from concourse import mybir
from concourse.alu_op_type import AluOpType as ALU

F32 = mybir.dt.float32
F32R = mybir.dt.float32r
I32 = mybir.dt.int32
ACT = mybir.ActivationFunctionType
AX = mybir.AxisListType

P = 128
TWO_PI = 6.283185


class Line:

    def __init__(self, sem):
        self.sem, self.value = sem, 0

    def mark(self, instruction, by=1):
        instruction.then_inc(self.sem, by)
        self.value += by
        return (self, self.value)


class Readers(dict):

    def __init__(self):
        self.held = set()

    def __setitem__(self, buffer, point):
        super().__setitem__(buffer, point)
        self.held.discard(buffer)


class Waits:

    def __init__(self):
        self.passed = {}

    def need(self, engine, *points):
        for point in points:
            if point is None:
                continue
            line, value = point
            key = (id(engine), id(line))
            if self.passed.get(key, 0) < value:
                engine.wait_ge(line.sem, value)
                self.passed[key] = value


def macaron(nc, x, w_mem, conv_k, w_q, theta, decay, anchor, score_scale, w_re, w_im, norm_scale,
            w_out, gate_w, w1, b1, w2, b2, sw1, sb1, sw2, sb2, out):
    B, T, D = x.shape
    E, _, H = w1.shape
    SH = sw1.shape[1]
    K, HH, N2 = w_re.shape
    M = theta.shape[4]
    KQ = w_q.shape[1] // (HH * M * 2)
    CW = conv_k.shape[0]
    KH = K * HH
    KC = D // P
    TB = T // P
    HALVES = KH // P
    EC = H // P
    SC = SH // P
    NV = N2 // 2
    VT = K * NV // P
    ND = decay.shape[0]
    KT = P // HH
    QUARTERS = 2 * HALVES
    QV = KT // 2 * NV
    VH = VT // HALVES
    KPQ = K // KQ
    QH = KQ // HALVES
    assert (P, T, D) == (128, 512, 512) and HH * M * 2 == P and K == 32 and CW == 4 and 2 * QV == 3 * P

    ctx = ExitStack()
    with ctx:
        def sb(name, shape, dt=F32):
            return ctx.enter_context(nc.sbuf_tensor(name, shape, dt))

        def line(name):
            return Line(ctx.enter_context(nc.semaphore(name)))

        NW = 2
        w1_ring = sb("w1_ring", [P, NW, 2, KC, H], F32R)
        w2_ring = sb("w2_ring", [P, NW, 2, EC, D], F32R)
        sw1_sb = sb("sw1_sb", [P, 2, KC, SH], F32R)
        sw2_sb = sb("sw2_sb", [P, 2, SC, D], F32R)
        gate_sb = sb("gate_sb", [P, KC, 2, E], F32R)
        gate_raw = sb("gate_raw", [P, KC, E])
        bias_sb = sb("bias_sb", [P, E * EC + SC])
        wmem_sb = sb("wmem_sb", [P, KC, KH + K])
        wq_sb = sb("wq_sb", [P, KC, KQ, 2, M, HH])
        wbd_sb = sb("wbd_sb", [P, QUARTERS, 2, 2 * P])
        wout_sb = sb("wout_sb", [P, VT, D])
        conv_sb = sb("conv_sb", [P, HALVES + 1, CW])
        theta_sb = sb("theta_sb", [P, HALVES, M])
        norm_sb = sb("norm_sb", [P, HALVES])
        scale_sb = sb("scale_sb", [K, 1])
        logw_sb = sb("logw_sb", [K, T])
        G0 = 2 * K
        BR = 3 * (E + 1)
        bias_parts = sb("bias_parts", [BR, 2, T], F32R)
        b2_sb = bias_parts[:, 0, :]
        ident = sb("ident", [P, P])
        rep_sb = sb("rep_sb", [K, KH])
        before = sb("before", [P, E, E])
        minus_half = sb("minus_half", [P, TB])
        half_pi = sb("half_pi", [P, 1])
        zero1 = sb("zero1", [P, 1])
        slope = sb("slope", [K, 8])

        xin = sb("xin", [P, TB, D])
        norms = {user: (sb(f"stats_{user}", [P, TB, 6]), sb(f"mv_{user}", [P, TB, 2]),
                        sb(f"rstd_{user}", [P, 3, TB])) for user in ("ffn", "attn")}
        xnT = sb("xnT", [P, 2, KC, T], F32R)
        NHB = 3
        hT = sb("hT", [P, NHB, T])
        NHP = 2
        hparts = sb("hparts", [P, NHP, 2, T], F32R)
        NGB = 2
        gateT = sb("gateT", [P, NGB, T])
        lg = sb("lg", [P, TB, E])
        cmp_a = sb("cmp_a", [P, TB, E, E])
        cmp_b = sb("cmp_b", [P, TB, E, E])
        rank = sb("rank", [P, TB, E])
        top = sb("top", [P, TB])
        ge = sb("ge", [P, TB, E])
        GC = G0 // 2
        gcols = sb("gcols", [P, TB, GC + E])
        NRES = TB
        res = sb("res", [P, NRES, D])

        kval = sb("kval", [P, HALVES, T])
        pwx = sb("pwx", [P, HALVES, T])
        few_rows = sb("few_rows", [P, 2, T])
        pw = few_rows[0:K, :, :]
        gT = bias_parts[:, 1, :]
        gate_rows = few_rows[G0 + GC:G0 + GC + E, 0, :]
        logitsT = few_rows[G0:G0 + 2 * E, 1, :]
        outT = sb("outT", [P, HALVES, 2, T])
        NQX = 2
        qx = sb("qx", [P, NQX, 2, T])
        core = sb("core", [P, 20 * 256])
        turn = core[:, 0:2 * T].rearrange("p (s t) -> p s t", s=2)
        trig = core[:, 2 * T:6 * T].rearrange("p (s c t) -> p s c t", s=2, c=2)
        run = core[:, 6 * T:8 * T].rearrange("p (c t) -> p c t", c=2)
        prod = core[:, 8 * T:10 * T].rearrange("p (c t) -> p c t", c=2)
        anT = core[:, 2 * T:6 * T].rearrange("p (c t) -> p c t", c=KC)
        ZP = T + CW - 1
        zT = core[:, 6 * T:6 * T + 2 * (ZP + 1)].rearrange("p (s t) -> p s t", s=2)
        qT = outT[:, 1, :, :]
        yT = core[:, 0:VT * T].rearrange("p (v t) -> p v t", v=VT)
        sil = core[:, VT * T:(VT + 2) * T].rearrange("p (s t) -> p s t", s=2)

        acc = ctx.enter_context(nc.psum_tensor("acc", [P, TB, D], F32))
        hps = ctx.enter_context(nc.psum_tensor("hps", [P, 2, T], F32))
        misc = ctx.enter_context(nc.psum_tensor("misc", [P, 2, T], F32))

        x1_dram = nc.dram_tensor("x1_rows", (B, T, D), F32).ap()
        x2_dram = nc.dram_tensor("x2_rows", (B, T, D), F32).ap()
        q_dram = nc.dram_tensor("q_cols", (KQ, M, HH, 2, T), F32)
        g_dram = nc.dram_tensor("gate_cols", (E, T), F32)
        w1_dram = nc.dram_tensor("w1_parts", (E, P, 2, KC, H), F32).ap()
        w2_dram = nc.dram_tensor("w2_parts", (E, P, 2, EC, D), F32).ap()
        w_dram = (w1_dram, w2_dram)

        pe, act, dve, pool = line("s_pe"), line("s_act"), line("s_dve"), line("s_pool")
        row_buffers = {"xin": xin, "res": res}
        l_res = [line(f"s_res{i}") for i in range(NRES)]
        l_rows = {"xin": [line(f"s_xin{i}") for i in range(TB)], "res": l_res}
        l_gst = line("s_gate_store")
        l_gate = [line(f"s_gate{i}") for i in range(NGB)]
        l_qst = [line(f"s_q_store{i}") for i in range(2)]
        l_qx = [line(f"s_qx{i}") for i in range(NQX)]
        l_out = [line(f"s_out_half{i}") for i in range(HALVES)]
        l_const = line("s_const")
        l_b2 = line("s_b2_low")
        l_shared = [line(f"s_shared_w{i}") for i in (1, 2)]
        l_attn = line("s_attn_weights")
        l_raw = [[line(f"s_raw{i}_{n}") for n in range(NW)] for i in (1, 2)]
        l_w = [[line(f"s_w{i}_{n}") for n in range(NW)] for i in (1, 2)]
        lines = [pe, act, dve, pool, *l_rows["xin"], *l_res, l_gst, *l_gate, *l_qst, *l_qx, *l_out, l_const,
                 l_b2,
                 *l_shared,
                 l_attn, *l_raw[0], *l_raw[1], *l_w[0], *l_w[1]]

        PARTS = ((0, 0), (0, 1), (1, 0))
        PE, VE, SE, GE, SP = nc.tensor, nc.vector, nc.scalar, nc.gpsimd, nc.sync
        waits = Waits()
        need = waits.need
        free = Readers()
        turns = {}

        def take(name, n):
            i = turns.get(name, 0)
            while (name, i % n) in free.held:
                i += 1
                assert i <= turns.get(name, 0) + n, f"no slot of {name} is free"
            turns[name] = i + 1
            free.held.add((name, i % n))
            return i % n

        def section_end():
            for ln in lines:
                need(SP, (ln, ln.value))
            nc.all_engine_barrier()
            nums = [ln.sem for ln in lines]
            for s in nums:
                GE.sem_clear(s)
            nc.all_engine_barrier()
            for ln in lines:
                ln.value = 0
            waits.passed.clear()
            free.clear()
            turns.clear()

        def section_joint():
            for ln in lines:
                need(SP, (ln, ln.value))
            for eng in (VE, SE, GE):
                for ln in (pe, act, dve, pool):
                    need(eng, (ln, ln.value))

        def row_tile(dram, b, tb):
            return bass.AP(dram.tensor, dram.offset + b * (T * D) + tb * P * D, [[D, P], [1, D]])

        def normalise(buf, src, b):
            xin = row_buffers[buf]
            stats, mv, rstd = norms["ffn" if buf == "xin" else "attn"]
            need(SP, free.get(buf))
            loaded = [ln.mark(SP.dma_start(xin[:, tb, :], row_tile(src, b, tb)), 16)
                      for tb, ln in enumerate(l_rows[buf])]
            yield
            for tb in range(TB):
                need(VE, loaded[tb])
                s = dve.mark(VE.bn_stats(stats[:, tb, :], xin[:, tb, :]))
            need(VE, s)
            for tb in range(TB):
                s = dve.mark(VE.bn_aggr(mv[:, tb, :], stats[:, tb, :]))
            need(GE, s)
            r, v, u = rstd[:, 0, :], rstd[:, 1, :], rstd[:, 2, :]
            need(GE, pool.mark(GE.tensor_scalar(v, mv[:, :, 1], 1e-5, None, ALU.add)))
            need(GE, pool.mark(GE.tensor_tensor(r, v, minus_half[:, :], ALU.pow)))
            need(GE, pool.mark(GE.tensor_tensor(u, r, r, ALU.mult)))
            need(GE, pool.mark(GE.tensor_tensor(u, u, v, ALU.mult)))
            need(GE, pool.mark(GE.tensor_scalar(u, u, -0.5, 1.5, ALU.mult, ALU.add)))
            rstd_ready = pool.mark(GE.tensor_tensor(r, r, u, ALU.mult))

            yield
            need(VE, rstd_ready)
            yield [dve.mark(VE.tensor_scalar(xin[:, tb, :], xin[:, tb, :], mv[:, tb, 0:1],
                                             rstd[:, 0, tb:tb + 1], ALU.subtract, ALU.mult))
                   for tb in range(TB)]

        def turn_tile(buf, tb, ready):
            xin = row_buffers[buf]
            bank = take("misc", 2)
            need(PE, ready, free.get(("misc", bank)))
            for c in range(KC):
                t = PE.transpose(misc[:, bank, c * P:(c + 1) * P], xin[:, tb, c * P:(c + 1) * P],
                                 ident[:, :])
            free[buf] = pe.mark(t)
            return bank, free[buf], misc[:, bank, :].rearrange("p (c t) -> p c t", c=KC)

        def turn_into(dst, tb, normalised):
            bank, turned, cols = turn_tile("res", tb, normalised[tb])
            need(SE, turned)
            free["misc", bank] = act.mark(SE.copy(dst[:, :, tb * P:(tb + 1) * P], cols))
            return free["misc", bank]

        def turn_into_parts(dst, tb, normalised):
            need(SE, free.get("xnT"))
            need(VE, free.get("xnT"))
            bank, turned, cols = turn_tile("xin", tb, normalised[tb])
            high, low = (dst[:, i, :, tb * P:(tb + 1) * P] for i in range(2))
            need(SE, turned)
            need(VE, act.mark(SE.copy(high, cols)))
            free["misc", bank] = dve.mark(VE.tensor_tensor(low, cols, high.bitcast(F32),
                                                           ALU.subtract))
            return free["misc", bank]

        def gates(xn_ready, result):
            bank = take("misc", 2)
            need(PE, xn_ready, free.get(("misc", bank)))
            for c in range(KC):
                PE.matmul(misc[0:2 * E, bank, :], gate_sb[:, c, :, :].rearrange("p i e -> p (i e)"),
                          xnT[:, 0, c, :], start=c == 0, stop=False)
                t = PE.matmul(misc[0:E, bank, :], gate_sb[:, c, 0, :], xnT[:, 1, c, :],
                              start=False, stop=c == KC - 1)
            need(VE, pe.mark(t), free.get("logitsT"))
            s = dve.mark(VE.tensor_copy(logitsT, misc[0:2 * E, bank, :]))
            free["misc", bank] = s
            yield
            bank = take("misc", 2)
            need(PE, s, free.get(("misc", bank)))
            for tb in range(TB):
                t = PE.transpose(misc[:, bank, tb * 2 * E:(tb + 1) * 2 * E],
                                 logitsT[:, tb * P:(tb + 1) * P],
                                 ident[G0:G0 + 2 * E, G0:G0 + 2 * E])
            free["logitsT"] = pe.mark(t)
            need(VE, free["logitsT"])
            halves = misc[:, bank, 0:TB * 2 * E].rearrange("p (t i e) -> p t i e", i=2, e=E)
            need(VE, dve.mark(VE.tensor_copy(lg[:, :, :], halves[:, :, 1, :])))
            s = dve.mark(VE.tensor_tensor(lg[:, :, :], lg[:, :, :], halves[:, :, 0, :], ALU.add))
            free["misc", bank] = s
            need(VE, s)
            other = lg[:, :, None, :].broadcast_to([P, TB, E, E])
            own = lg[:, :, :, None].broadcast_to([P, TB, E, E])
            low = before[:, None, :, :].broadcast_to([P, TB, E, E])
            dve.mark(VE.tensor_tensor(cmp_a[:, :, :, :], other, own, ALU.is_gt))
            dve.mark(VE.tensor_reduce(top[:, :], lg[:, :, :], AX.X, ALU.max))
            need(VE, dve.mark(VE.tensor_tensor(cmp_b[:, :, :, :], other, own, ALU.is_equal)))
            need(VE, dve.mark(VE.tensor_tensor(cmp_b[:, :, :, :], cmp_b[:, :, :, :], low, ALU.mult)))
            s = dve.mark(VE.tensor_tensor(ge[:, :, :], lg[:, :, :],
                                          top[:, :, None].broadcast_to([P, TB, E]), ALU.subtract))
            need(SE, s)
            e = act.mark(SE.activation(ge[:, :, :], ge[:, :, :], ACT.Exp))
            yield
            need(VE, dve.mark(VE.tensor_tensor(cmp_a[:, :, :, :], cmp_a[:, :, :, :],
                                               cmp_b[:, :, :, :], ALU.add)))
            need(VE, dve.mark(VE.tensor_reduce(rank[:, :, :], cmp_a[:, :, :, :], AX.X, ALU.add)))
            need(VE, dve.mark(VE.tensor_scalar(rank[:, :, :], rank[:, :, :], 1.5, None, ALU.is_lt)))
            need(VE, e)
            need(VE, dve.mark(VE.tensor_tensor(ge[:, :, :], ge[:, :, :], rank[:, :, :], ALU.mult)))
            need(VE, dve.mark(VE.tensor_reduce(top[:, :], ge[:, :, :], AX.X, ALU.add)))
            need(VE, dve.mark(VE.reciprocal(top[:, :], top[:, :])))
            whole = gcols[:, :, GC:GC + E]
            need(VE, dve.mark(VE.tensor_tensor(whole, ge[:, :, :],
                                               top[:, :, None].broadcast_to([P, TB, E]), ALU.mult)))
            high2 = gcols[:, :, 0:2 * (E + 1)].rearrange("p t (a e) -> p t a e", a=2)[:, :, :, 0:E]
            need(VE, dve.mark(VE.tensor_copy(high2.bitcast(F32R),
                                             whole[:, :, None, :].broadcast_to([P, TB, 2, E]))))
            low = gcols[:, :, 2 * (E + 1):2 * (E + 1) + E]
            s = dve.mark(VE.tensor_tensor(low, whole, gcols[:, :, 0:E], ALU.subtract))
            yield
            bank = take("misc", 2)
            need(PE, s, free.get(("misc", bank)))
            for tb in range(TB):
                t = PE.transpose(misc[0:GC + E, bank, tb * P:(tb + 1) * P], gcols[:, tb, :],
                                 ident[:, :])
            t = pe.mark(t)
            need(SE, t, free.get("g_stored"))
            rows_ready = act.mark(SE.copy(gate_rows, misc[GC:GC + E, bank, :]))
            need(VE, rows_ready, free.get("gT"))
            gT_ready = dve.mark(VE.tensor_copy(gT, misc[0:BR, bank, :]))
            free["misc", bank] = gT_ready
            need(SP, rows_ready, free.get("g_dram"))
            stored = l_gst.mark(SP.dma_start(g_dram.ap(), gate_rows), 16)
            free["g_stored"] = stored
            result["gT"], result["stored"] = gT_ready, stored
            yield

        fetched = {}

        def ring(i, slot):
            return (w1_ring if i == 0 else w2_ring)[:, slot, :, :, :]

        def fetch(e, i):
            slot = e % NW
            src = (w1 if i == 0 else w2)[e].rearrange("(c p) n -> p c n", p=P)
            need(SP, free.get(("raw", i, slot)))
            fetched[e, i] = l_raw[i][slot].mark(SP.dma_start(raw_w(slot)[i], src), 16)

        def raw_weights(e, i):
            slot = e % NW
            raw, there = raw_w(slot)[i], fetched[e, i]
            high, low = ring(i, slot)[:, 0, :, :], ring(i, slot)[:, 1, :, :]
            stored = (l_w[i][slot], l_w[i][slot].value)
            need(SE, there, free.get(("w", i, slot)), stored)
            need(VE, there, free.get(("w", i, slot)), stored)
            need(VE, act.mark(SE.copy(high, raw)))
            done = dve.mark(VE.tensor_tensor(low, raw, high.bitcast(F32), ALU.subtract))
            free["raw", i, slot] = done
            if e + NW < E:
                fetch(e + NW, i)
            need(SP, done)
            l_w[i][slot].mark(SP.dma_start(w_dram[i][e], ring(i, slot).bitcast(F32)), 16)
            return done

        def load_weights(e, i):
            slot = e % NW
            need(SP, free.get(("w", i, slot)))
            return l_w[i][slot].mark(SP.dma_start(ring(i, slot).bitcast(F32), w_dram[i][e]), 16)

        TILES = [("shared", j) for j in range(SC)] + [("routed", j) for j in range(E * EC)]
        NT = len(TILES)
        SHARE = {1: 0.75, 2: 1.0}
        LOAD_TIME, STATS_TIME, NORM_TIME = 1.0, 4.0, 1.0
        NORM_LEAD = 3
        LAG = 3
        GATE_WORK = 3

        def ffn(jobs, turned=False, following=None, started=None):
            hidden = {}
            state = [{} for _ in jobs]
            total = NT * len(jobs)

            def gate(k):
                q, n = divmod(k, NT)
                kind, j = TILES[n]
                if kind == "shared":
                    return
                e = j // EC
                slot, ready = hidden[k]
                g, gate_there = state[q]["gate"][e]
                need(VE, ready, gate_there)
                ready = dve.mark(VE.tensor_tensor(hT[:, slot, :], hT[:, slot, :], gateT[:, g, :],
                                                  ALU.mult))
                free["gateT", g] = ready
                hidden[k] = (slot, ready)

            def high_part(k):
                slot, ready = hidden[k]
                need(SE, ready, free.get(("hparts", k % NHP)))
                high_there = act.mark(SE.copy(hparts[:, k % NHP, 0, :], hT[:, slot, :]))
                hidden[k] = (slot, high_there)

            def low_part(k):
                slot, high_there = hidden[k]
                high, low = hparts[:, k % NHP, 0, :], hparts[:, k % NHP, 1, :]
                need(VE, high_there, free.get(("hparts", k % NHP)))
                s = dve.mark(VE.tensor_tensor(low, hT[:, slot, :], high.bitcast(F32), ALU.subtract))
                free["hT", slot] = s
                hidden[k] = s

            def follow(q, e, i, used):
                free["w", i, e % NW] = used
                if e + NW < E:
                    state[q]["w", e + NW, i] = jobs[q][3](e + NW, i)
                elif q + 1 < len(jobs):
                    state[q + 1]["w", e + NW - E, i] = jobs[q + 1][3](e + NW - E, i)

            def columns(st, k, beside=lambda: None):
                normalised = next(st["norm"])
                for tb in range(TB):
                    if tb == TB // 2:
                        beside()
                    st["xn"] = turn_into_parts(xnT, tb, normalised)

            def lagging(k):
                gate(k - 1)
                high_part(k - 2)
                accumulate(k - LAG)

            def accumulate(k):
                q, n = divmod(k, NT)
                kind, j = TILES[n]
                src, dst, b, provide = jobs[q]
                p = k % NHP
                if n == NT - 1:
                    loaded = [load_rows(src, b, tb) for tb in range(TB)]
                if n == SC:
                    need(PE, state[q]["gT"])
                    for tb in range(TB):
                        t = PE.matmul(acc[:, tb, :], gT[:, tb * P:(tb + 1) * P], b2_sb,
                                      start=False, stop=False)
                    free["gT"] = pe.mark(t)
                need(PE, hidden.pop(k))
                if kind == "routed":
                    need(PE, state[q]["w", j // EC, 1])
                for tb in range(TB):
                    if n == 0:
                        need(PE, free.get(("acc", tb)))
                    for i, (hp, wp) in enumerate(PARTS):
                        w = sw2_sb[:, wp, j, :] if kind == "shared" else \
                            w2_ring[:, (j // EC) % NW, wp, j % EC, :]
                        t = PE.matmul(acc[:, tb, :], hparts[:, p, hp, tb * P:(tb + 1) * P], w,
                                      start=n == 0 and i == 0, stop=n == NT - 1 and i == 2)
                done = pe.mark(t)
                free["hparts", p] = done
                if kind == "routed" and j % EC == EC - 1:
                    follow(q, j // EC, 1, done)
                if n == NT - 1:
                    for tb in range(TB):
                        free["acc", tb] = store_rows(loaded[tb], dst, b, tb, acc[:, tb, :],
                                                     done, 0.5)

            if turned:
                state[0]["xn"] = None
            else:
                state[0]["norm"] = started or normalise("xin", jobs[0][0], jobs[0][2])
                if started is None:
                    next(state[0]["norm"])
            for e in range(NW):
                for i in range(2):
                    state[0]["w", e, i] = jobs[0][3](e, i)
            yield 0.0
            if not turned and started is None:
                next(state[0]["norm"])
                yield 3.0
            for k in range(total + LAG):
                q, n = divmod(k, NT)
                if k >= LAG:
                    low_part(k - LAG)
                if k < total:
                    st = state[q]
                    if n == 0:
                        if k >= 1:
                            columns(st, k, lambda: lagging(k))
                        elif not turned:
                            columns(st, k)
                        st["gates"] = gates(st["xn"], st)
                        next(st["gates"])
                        st["gate"] = {}
                    kind, j = TILES[n]
                    e = j // EC
                    if kind == "routed" and j % EC == 0:
                        g = take("gateT", NGB)
                        need(SP, st["stored"], free.get(("gateT", g)))
                        st["gate"][e] = (g, l_gate[g].mark(
                            SP.dma_start(gateT[:, g, :], bass.AP(g_dram, e * T, [[0, P], [1, T]])), 16))
                        free["g_dram"] = st["gate"][e][1]
                    bank = take("hps", 2)
                    need(PE, st["xn"], free.get(("hps", bank)))
                    if kind == "routed":
                        need(PE, st["w", e, 0])
                    for c in range(KC):
                        for i, (wp, xp) in enumerate(PARTS):
                            w = sw1_sb[:, wp, c, j * P:(j + 1) * P] if kind == "shared" else \
                                w1_ring[:, e % NW, wp, c, (j % EC) * P:(j % EC + 1) * P]
                            t = PE.matmul(hps[:, bank, :], w, xnT[:, xp, c, :],
                                          start=c == 0 and i == 0, stop=c == KC - 1 and i == 2)
                    made = pe.mark(t)
                    free["xnT"] = made
                    if kind == "routed" and j % EC == EC - 1:
                        follow(q, e, 0, made)
                yield 2.55
                late = n == 0 and 0 < k < total
                if not late:
                    if 0 <= k - 1 < total:
                        gate(k - 1)
                    if 0 <= k - 2 < total:
                        high_part(k - 2)
                if k < total:
                    slot = take("hT", NHB)
                    need(SE, made, free.get(("hT", slot)))
                    at = E * EC + j if kind == "shared" else j
                    bias = bias_sb[:, at:at + 1]
                    ready = act.mark(SE.activation(hT[:, slot, :], hps[:, bank, :], ACT.Gelu,
                                                   bias=bias))
                    free["hps", bank] = ready
                    hidden[k] = (slot, ready)
                if k >= LAG and not late:
                    accumulate(k - LAG)
                if k < total and n < GATE_WORK:
                    next(st["gates"])
                if k < total and n == NT // 2 - NORM_LEAD:
                    if q + 1 < len(jobs):
                        coming = normalise("xin", jobs[q + 1][0], jobs[q + 1][2])
                        state[q + 1]["norm"] = coming
                    elif following is not None:
                        coming = normalise("xin", *following)
                        last = {"norm": coming}
                    else:
                        coming = None
                if k < total and n in (NT // 2 - NORM_LEAD, NT // 2) and coming:
                    next(coming)
                if k == total and following is not None:
                    columns(last, k)
                yield 2.55

        def load_rows(src, b, tb):
            s = take("res", NRES)
            need(SP, free.get(("res", s)))
            return s, l_res[s].mark(SP.dma_start(res[:, s, :], row_tile(src, b, tb)), 16)

        def store_rows(slot_loaded, dst, b, tb, result, ready, factor):
            s, loaded = slot_loaded
            need(VE, ready, loaded)
            summed = dve.mark(VE.scalar_tensor_tensor(res[:, s, :], result, factor, res[:, s, :],
                                                      ALU.mult, ALU.add))
            need(SP, summed)
            free["res", s] = l_res[s].mark(SP.dma_start(row_tile(dst, b, tb), res[:, s, :]), 16)
            return summed

        def spread(half, i, *ready):
            bank = take("misc", 2)
            need(PE, *ready, free.get(("misc", bank)))
            return bank, pe.mark(PE.matmul(misc[:, bank, :], rep_sb[:, half * P:(half + 1) * P],
                                           pw[:, i, :], start=True, stop=True))

        def attention_inputs(norm):
            yield LOAD_TIME
            next(norm)
            yield STATS_TIME
            normalised = next(norm)
            yield NORM_TIME
            for tb in range(TB):
                an_ready = turn_into(anT, tb, normalised)
            for s in range(NRES):
                free["res", s] = free["res"]
            need(PE, (l_attn, l_attn.value))
            convolved = {}

            def memory_input(turn, i):
                rowsn = P if i < HALVES else K
                bank = take("misc", 2)
                need(PE, an_ready, free.get(("misc", bank)))
                for c in range(KC):
                    t = PE.matmul(misc[0:rowsn, bank, :], wmem_sb[:, c, i * P:i * P + rowsn],
                                  anT[:, c, :], start=c == 0, stop=c == KC - 1)
                z = zT[0:rowsn, turn % 2, :]
                free["anT"] = pe.mark(t)
                need(SE, free["anT"], convolved.get(turn - 2))
                need(VE, dve.mark(VE.memset(z[:, 0:CW - 1], 0.0)))
                s = act.mark(SE.copy(z[:, CW - 1:ZP], misc[0:rowsn, bank, :]))
                free["misc", bank] = s
                need(VE, s)
                o = kval[:, i, :] if i < HALVES else pw[:, 0, :]
                s = dve.mark(VE.tensor_scalar(o, z[:, 0:T], conv_sb[0:rowsn, i, 0:1], None, ALU.mult))
                for k in range(1, CW):
                    need(VE, s)
                    s = dve.mark(VE.scalar_tensor_tensor(o, z[:, k:k + T],
                                                         conv_sb[0:rowsn, i, k:k + 1], o,
                                                         ALU.mult, ALU.add))
                convolved[turn] = free["kval"] = s
                return s

            def query_input(q):
                bank = take("misc", 2)
                need(PE, free.get(("misc", bank)))
                for c in range(KC):
                    t = PE.matmul(misc[:, bank, :], wq_sb[:, c, q, :, :, :].rearrange("p a b c -> p (a b c)"),
                                  anT[:, c, :], start=c == 0, stop=c == KC - 1)
                t = pe.mark(t)
                free["anT"] = t
                need(SE, t, free.get(("qT", q % 2)))
                s = act.mark(SE.copy(qT[:, q % 2, :], misc[:, bank, :]))
                free["misc", bank] = s
                need(SP, s)
                free["qT", q % 2] = l_qst[q % 2].mark(
                    SP.dma_start(bass.AP(q_dram, q * P * T, [[T, 2], [2 * T, M * HH], [1, T]]),
                                 qT[:, q % 2, :]), 16)

            s = memory_input(0, HALVES)
            yield 1.5
            for q in range(QH):
                query_input(q)
                yield 1.5
            need(VE, s)
            p, den = pw[:, 0, :], pw[:, 1, :]
            need(VE, dve.mark(VE.tensor_scalar(p, p, scale_sb[:, 0:1], 20.0, ALU.mult, ALU.min)))
            s = dve.mark(VE.scalar_tensor_tensor(p, p, -20.0, logw_sb[:, :], ALU.max, ALU.add))
            need(SE, s)
            weights = act.mark(SE.activation(p, p, ACT.Exp))
            memory_input(1, 0)
            yield 1.5
            for q in range(QH, KQ):
                query_input(q)
                yield 1.5
            need(VE, weights)
            need(VE, dve.mark(VE.tensor_tensor_scan(den, p, zero1[0:K, 0:1].broadcast_to([K, T]), 0.0,
                                                    ALU.add, ALU.add)))
            need(VE, dve.mark(VE.tensor_scalar(den, den, 1e-4, None, ALU.max)))
            memory_input(2, 1)
            yield 1.5
            for half in range(HALVES):
                bank, t = spread(half, 0, weights)
                need(SE, t)
                free["misc", bank] = act.mark(SE.copy(pwx[:, half, :], misc[:, bank, :]))
            free["spread"] = free["misc", bank]
            yield 1.0

        def attention_core(b):
            steps = [(half, m) for half in range(HALVES) for m in range(M)]
            front = {}

            def load_queries(n):
                half, m = steps[n]
                s = n % NQX
                need(SP, free.get(("qx", s)), *[(ln, ln.value) for ln in l_qst])
                for g in range(QH):
                    q = half * QH + g
                    src = bass.AP(q_dram, q * P * T + m * HH * 2 * T,
                                  [[0, KPQ], [2 * T, HH], [1, 2 * T]])
                    at = l_qx[s].mark(SP.dma_start(qx[g * KPQ * HH:(g + 1) * KPQ * HH, s, :, :], src), 16)
                front[n, "q"] = at

            def phases(n):
                half, m = steps[n]
                s = n % 2
                f, nearest = turn[:, s, :], prod_int(s)
                th = theta_sb[:, half, m:m + 1]
                need(VE, free.get(("turn", s)), free["kval"])
                r = dve.mark(VE.tensor_scalar(nearest, kval[:, half, :], th, None, ALU.mult))
                need(VE, r)
                r = dve.mark(VE.scalar_tensor_tensor(f, kval[:, half, :], th, nearest,
                                                     ALU.mult, ALU.subtract))
                need(SE, r, free.get(("trig", s)), free.get("anT"))
                a = act.mark(SE.activation(trig[:, s, 0, :], f, ACT.Abs))
                act.mark(SE.activation(trig[:, s, 1, :], f, ACT.Sin, scale=TWO_PI))
                need(SE, a)
                a = act.mark(SE.activation(trig[:, s, 0, :], trig[:, s, 0, :], ACT.Sin,
                                           scale=-TWO_PI, bias=half_pi[:, 0:1]))
                free["turn", s] = a
                front[n] = a

            def prod_int(s):
                return turn[:, s, :].bitcast(I32)

            def sums(n):
                half, m = steps[n]
                s, qs = n % 2, n % NQX
                cs = trig[:, s, :, :]
                need(VE, front[n], free["spread"])
                w = dve.mark(VE.tensor_tensor(cs, cs, pwx[:, half, None, :].broadcast_to([P, 2, T]),
                                              ALU.mult))
                yield 1.6
                need(VE, w)
                for c in range(2):
                    w = dve.mark(VE.tensor_tensor_scan(run[:, c, :], trig[:, s, c, :],
                                                       zero1[:, 0:1].broadcast_to([P, T]), 0.0,
                                                       ALU.add, ALU.add))
                free["trig", s] = w
                yield 1.6
                if n + 2 < len(steps):
                    phases(n + 2)
                need(VE, w, front[n, "q"])
                w = dve.mark(VE.tensor_tensor(prod[:, :, :], run[:, :, :], qx[:, qs, :, :], ALU.mult))
                yield 1.6
                need(VE, w)
                back = bass.AP(run.tensor, run.offset + T, [list(run.ap[0]), [-T, 2], [1, T]])
                w3 = dve.mark(VE.tensor_tensor(qx[:, qs, :, :], back, qx[:, qs, :, :], ALU.mult))
                yield 1.6
                re, im = outT[:, half, 0, :], outT[:, half, 1, :]
                if m == 0:
                    dve.mark(VE.tensor_tensor(re, prod[:, 0, :], prod[:, 1, :], ALU.add))
                    need(VE, w3)
                    w3 = dve.mark(VE.tensor_tensor(im, qx[:, qs, 0, :], qx[:, qs, 1, :], ALU.subtract))
                else:
                    w = dve.mark(VE.tensor_tensor(prod[:, 0, :], prod[:, 0, :], prod[:, 1, :], ALU.add))
                    need(VE, w3)
                    w3 = dve.mark(VE.tensor_tensor(qx[:, qs, 0, :], qx[:, qs, 0, :], qx[:, qs, 1, :],
                                                   ALU.subtract))
                    yield 1.6
                    need(VE, w)
                    dve.mark(VE.tensor_tensor(re, re, prod[:, 0, :], ALU.add))
                    need(VE, w3)
                    w3 = dve.mark(VE.tensor_tensor(im, im, qx[:, qs, 0, :], ALU.add))
                free["qx", qs] = w3
                yield 1.6
                if m == M - 1:
                    bank, t = spread(half, 1, free["den"])
                    need(VE, t, w3)
                    for part in range(2):
                        w3 = dve.mark(VE.scalar_tensor_tensor(
                            qx[:, qs, part, :], outT[:, half, part, :], norm_sb[:, half:half + 1],
                            misc[:, bank, :], ALU.mult, ALU.mult))
                    free["misc", bank] = w3
                    need(SP, w3)
                    for i in range(2):
                        for part in range(2):
                            moved = l_out[half].mark(SP.dma_start(
                                outT[part * 64:(part + 1) * 64, half, i, :],
                                qx[i * 64:(i + 1) * 64, qs, part, :]), 16)
                    free["qx", qs] = moved
                    free["outT", half] = moved
                    yield 1.8

            load_queries(0)
            phases(0)
            phases(1)
            free["den"] = dve.mark(VE.reciprocal(pw[:, 1, :], pw[:, 1, :]))
            yield 0.0
            for n in range(len(steps)):
                if n + 1 < len(steps):
                    load_queries(n + 1)
                yield 1.6
                yield from sums(n)

        def attention_output(b):
            core_done = free["outT", HALVES - 1]
            psum = {"misc": misc, "hps": hps}
            for v in range(VT):
                half, j = v // VH, v % VH
                sources = {0: [(0, 0)], 1: [(0, 1), (1, 0)], 2: [(1, 1)]}[j]
                banks = []
                for vg, pair in enumerate(("misc", "hps")):
                    bank = take(pair, 2)
                    banks.append(bank)
                    need(PE, free["outT", half], free.get((pair, bank)))
                    for i, (quarter, tile) in enumerate(sources):
                        w = wbd_sb[:, 2 * half + quarter, vg, tile * P:(tile + 1) * P]
                        t = PE.matmul(psum[pair][:, bank, :], w, outT[:, half, quarter, :],
                                      start=i == 0, stop=i == len(sources) - 1)
                    t = pe.mark(t)
                need(SE, t, core_done, free.get(("sil", v % 2)))
                s = act.mark(SE.activation(sil[:, v % 2, :], hps[:, banks[1], :], ACT.Silu))
                free["hps", banks[1]] = s
                yield 1.7
                need(VE, s)
                s = dve.mark(VE.tensor_tensor(yT[:, v, :], misc[:, banks[0], :], sil[:, v % 2, :],
                                              ALU.mult))
                free["misc", banks[0]] = s
                free["sil", v % 2] = s
                yield 1.7
            for tb in range(TB):
                loaded = load_rows(x1_dram, b, tb)
                bank = take("misc", 2)
                need(PE, s, free.get(("misc", bank)))
                for v in range(VT):
                    t = PE.matmul(misc[:, bank, :], yT[:, v, tb * P:(tb + 1) * P], wout_sb[:, v, :],
                                  start=v == 0, stop=v == VT - 1)
                free["misc", bank] = store_rows(loaded, x2_dram, b, tb, misc[:, bank, :],
                                                pe.mark(t), 1.0)
                yield 5.1

        def chain(*parts):
            for p in parts:
                yield from p

        def together(a, f, share=1.0):
            ta = tf = 0.0
            live = [a, f]
            while live:
                g = live[0] if len(live) == 1 else (a if ta <= tf else f)
                try:
                    c = next(g)
                except StopIteration:
                    live.remove(g)
                    continue
                if g is a:
                    ta += c * share
                else:
                    tf += c

        def section(b, second_ffn, first_ffn):
            jobs = []
            if first_ffn:
                jobs.append((x, x1_dram, b + 1, load_weights))
            if second_ffn:
                jobs.append((x2_dram, out, b - 1, load_weights))
            following = (x, min(b + 2, B - 1) if isinstance(b, int) else B - 1) if first_ffn else None
            other = ffn(jobs, turned=first_ffn, following=following)
            norm = normalise("res", x1_dram, b)
            next(norm)
            next(other)
            together(chain(attention_inputs(norm), attention_core(b), attention_output(b)),
                     other, SHARE[len(jobs)])
            if first_ffn:
                section_end()
            else:
                section_joint()

        def load(ln, dst, src, eng=SP):
            return ln.mark(eng.dma_start(dst, src), 16)

        def turned_rows(n, dst, *ready):
            bank = take("misc", 2)
            need(PE, *ready, free.get(("misc", bank)))
            t = pe.mark(PE.transpose(misc[:, bank, 0:n], vec_rows[0:n, :], ident[0:n, 0:n]))
            need(VE, t)
            free["misc", bank] = dve.mark(VE.tensor_copy(dst, misc[:, bank, 0:n]))
            return free["misc", bank]

        core_raw = core[:, 0:4096].rearrange("p (i n) -> p i n", i=2)
        core_rest = core[:, 4096:5120]
        vec_rows = core_rest[:, 0:P]
        w_raw = core_rest[:, P:P + QUARTERS * N2].rearrange("p (g n) -> p g n", g=QUARTERS)
        wq_raw = core_rest[:, P + QUARTERS * N2:P + QUARTERS * N2 + KQ * P]

        def raw_w(slot):
            r = core_raw[:, slot, :].rearrange("p (i n) -> p i n", i=2)
            return (r[:, 0, :].rearrange("p (c h) -> p c h", c=KC),
                    r[:, 1, :].rearrange("p (c d) -> p c d", c=EC))

        def pg(i):
            return pool.mark(i)

        ctx.enter_context(nc.allow_non_contiguous_dma(reason="small vectors, loaded once"))
        pg(GE.memset(minus_half[:, :], -0.5))
        need(GE, pg(GE.memset(ident[:, :], 0.0)))
        ident_ready = pg(GE.affine_select(out=ident[:, :], in_=ident[:, :], compare_op=ALU.not_equal,
                                          fill=1.0, base=0, pattern=[[-1, P]], channel_multiplier=1))
        norm0 = normalise("xin", x, 0)
        next(norm0)
        job0 = ffn([(x, x1_dram, 0, raw_weights)], following=(x, 1), started=norm0)
        load(l_const, gate_raw[:, :, :], gate_w.rearrange("(c p) e -> p c e", p=P), SE)
        load(l_const, vec_rows[0:E * EC, :], b1.rearrange("e (c p) -> (e c) p", p=P), SE)
        load(l_const, vec_rows[E * EC:E * EC + SC, :], sb1.rearrange("(c p) -> c p", p=P), SE)
        b2_raw, b2_rest = outT[0:BR, 0, 0, :], gT
        for i in range(3):
            load(l_const, b2_raw[i * (E + 1):i * (E + 1) + E, :], b2, SE)
            load(l_const, b2_raw[i * (E + 1) + E:(i + 1) * (E + 1), :],
                 sb2.rearrange("(a d) -> a d", a=1), SE)
        load(l_shared[0], core_raw[:, 0, :].rearrange("p (c h) -> p c h", c=KC),
             sw1.rearrange("(c p) h -> p c h", p=P), SE)
        load(l_shared[1], core_raw[:, 1, :].rearrange("p (c d) -> p c d", c=SC),
             sw2.rearrange("(c p) d -> p c d", p=P), SE)

        pg(GE.memset(half_pi[:, :], math.pi / 2))
        pg(GE.memset(zero1[:, :], 0.0))
        pg(GE.memset(gcols[:, :, 0:2 * (E + 1)], 1.0))
        pg(GE.memset(gcols[:, :, 2 * (E + 1):GC + E], 0.0))
        pg(GE.memset(before[:, :, :], 1.0))
        need(GE, pg(GE.memset(rep_sb[:, :], 1.0)))
        pg(GE.affine_select(out=before[:, :, :], in_=before[:, :, :], compare_op=ALU.is_gt, fill=0.0,
                            base=0, pattern=[[1, E], [-1, E]], channel_multiplier=0))
        need(GE, pg(GE.affine_select(out=rep_sb[:, :], in_=rep_sb[:, :], compare_op=ALU.is_ge, fill=0.0,
                                     base=0, pattern=[[1, KH]], channel_multiplier=-HH)))
        consts = pg(GE.affine_select(out=rep_sb[:, :], in_=rep_sb[:, :], compare_op=ALU.is_ge, fill=0.0,
                                     base=HH - 1, pattern=[[-1, KH]], channel_multiplier=HH))
        need(PE, ident_ready, consts)
        need(VE, consts)
        need(SE, consts)
        for eng in (PE, SE, VE):
            need(eng, (l_const, l_const.value))
        turned_rows(E * EC + SC, bias_sb[:, :])
        next(norm0)
        need(VE, dve.mark(VE.tensor_copy(b2_sb, b2_raw)))
        need(SP, dve.mark(VE.tensor_tensor(b2_rest, b2_raw, b2_sb.bitcast(F32), ALU.subtract)))
        b2_ready = load(l_b2, b2_sb[E + 1:2 * (E + 1), :].bitcast(F32),
                        b2_rest[E + 1:2 * (E + 1), :].bitcast(F32))
        gate_parts = gate_sb[:, :, :, :].rearrange("p c i e -> p i c e")
        for raw, dst, there in ((gate_raw[:, :, :], gate_parts, None),
                                (core_raw[:, 0, :].rearrange("p (c h) -> p c h", c=KC), sw1_sb,
                                 (l_shared[0], 16)),
                                (core_raw[:, 1, :].rearrange("p (c d) -> p c d", c=SC), sw2_sb,
                                 (l_shared[1], 16))):
            need(SE, there)
            need(VE, there)
            need(VE, act.mark(SE.copy(dst[:, 0, :, :], raw)))
            s = dve.mark(VE.tensor_tensor(dst[:, 1, :, :], raw, dst[:, 0, :, :].bitcast(F32),
                                          ALU.subtract))
            if dst is not gate_parts:
                for i in range(2):
                    slot = 0 if dst is sw1_sb else 1
                    free["raw", i, slot] = s
                    fetch(slot, i)
        need(PE, s, b2_ready)
        need(SE, s)

        def attention_weights():
            for i in range(2):
                load(l_attn, w_raw[i * 64:(i + 1) * 64, :, :],
                     (w_re, w_im)[i].rearrange("(g k) h n -> (k h) g n", g=QUARTERS))
            load(l_attn, theta_sb[:, :, :], theta.rearrange("a b (g k) h m -> (a b k h) g m", g=HALVES))
            load(l_attn, norm_sb[:, :], norm_scale.rearrange("a b (g k) h -> (a b k h) g", g=HALVES))
            load(l_attn, scale_sb[:, :], score_scale.rearrange("(p a) -> p a", a=1))
            load(l_attn, slope[0:ND, 0:1], decay.rearrange("(p a) -> p a", a=1))
            load(l_attn, slope[ND:K, 0:1], anchor.rearrange("(p a) -> p a", a=1))
            small = (l_attn, l_attn.value)
            yield 20.0
            dist, posn = kval[0:K, 0, :], kval[0:K, 1, :]
            pg(GE.iota(dist, pattern=[[-1, T]], base=T - 1, channel_multiplier=0,
                       allow_small_or_imprecise_dtypes=True))
            need(GE, pg(GE.iota(posn, pattern=[[1, T]], base=0, channel_multiplier=0,
                                allow_small_or_imprecise_dtypes=True)))
            pg(GE.affine_select(out=dist, in_=dist, compare_op=ALU.is_gt, fill=0.0, base=ND,
                                pattern=[[0, T]], channel_multiplier=-1))
            dists = pg(GE.affine_select(out=posn, in_=posn, compare_op=ALU.is_ge, fill=0.0, base=-ND,
                                        pattern=[[0, T]], channel_multiplier=1))
            need(GE, small)
            for g in range(QUARTERS):
                zeros = slice(QV, 2 * P) if g % 2 == 0 else slice(0, 2 * P - QV)
                need(GE, (pool, pool.value))
                need(GE, pg(GE.memset(wbd_sb[:, g, :, zeros], 0.0)))
                for part in range(2):
                    ps = slice(part * 64, (part + 1) * 64)
                    for vg in range(2):
                        at = g % 2 * (2 * P - QV)
                        o = wbd_sb[ps, g, vg, at:at + QV].rearrange("p (k n) -> p k n", n=NV)
                        i_ = w_raw[ps, g, None, vg * NV:(vg + 1) * NV]\
                            .broadcast_to([64, KT // 2, NV])
                        need(GE, pg(GE.affine_select(out=o, in_=i_, compare_op=ALU.is_ge, fill=0.0,
                                                     base=0, pattern=[[-HH, KT // 2], [0, NV]],
                                                     channel_multiplier=1)))
                        need(GE, pg(GE.affine_select(out=o, in_=o, compare_op=ALU.is_ge, fill=0.0,
                                                     base=HH - 1, pattern=[[HH, KT // 2], [0, NV]],
                                                     channel_multiplier=-1)))
            need(VE, small)
            dve.mark(VE.tensor_scalar(theta_sb[:, :, :], theta_sb[:, :, :], 1 / (2 * math.pi), None,
                                      ALU.mult))
            col = [slope[:, i:i + 1] for i in range(8)]
            need(VE, dve.mark(VE.tensor_scalar(col[1], col[0], -1.0, None, ALU.mult)))
            s = dve.mark(VE.tensor_tensor(col[1], col[0], col[1], ALU.min))
            need(SE, s)
            e = act.mark(SE.activation(col[2], col[1], ACT.Exp))
            yield 5.0
            need(VE, e)
            need(VE, dve.mark(VE.tensor_scalar(col[3], col[2], 2.0, None, ALU.add)))
            need(VE, dve.mark(VE.reciprocal(col[3], col[3])))
            need(VE, dve.mark(VE.tensor_tensor(col[3], col[2], col[3], ALU.mult)))
            need(VE, dve.mark(VE.tensor_tensor(col[4], col[3], col[3], ALU.mult)))
            need(VE, dve.mark(VE.memset(col[5], 1.0 / 17)))
            yield 5.0
            for d in range(15, 0, -2):
                need(VE, dve.mark(VE.tensor_scalar(col[5], col[5], col[4], 1.0 / d, ALU.mult, ALU.add)))
            yield 5.0
            need(VE, dve.mark(VE.tensor_tensor(col[5], col[5], col[3], ALU.mult)))
            need(VE, dve.mark(VE.tensor_scalar(col[6], col[0], 0.0, None, ALU.max)))
            need(VE, dve.mark(VE.scalar_tensor_tensor(col[7], col[5], 2.0, col[6], ALU.mult, ALU.add)))
            need(VE, dve.mark(VE.tensor_scalar(col[7], col[7], -1.0, None, ALU.mult)))
            need(VE, dists)
            need(VE, dve.mark(VE.tensor_tensor(dist, dist, posn, ALU.add)))
            dve.mark(VE.tensor_scalar(logw_sb[:, :], dist, col[7], None, ALU.mult))
            yield 5.0
            for i in range(HALVES + 1):
                rowsn = P if i < HALVES else K
                need(SP, (pe, pe.value))
                there = load(l_attn, vec_rows[0:CW, 0:rowsn], conv_k[:, 0, i * P:i * P + rowsn])
                yield 5.0
                bank = take("misc", 2)
                need(PE, there, free.get(("misc", bank)))
                t = pe.mark(PE.transpose(misc[0:rowsn, bank, 0:CW], vec_rows[0:CW, 0:rowsn],
                                         ident[0:CW, 0:CW]))
                need(VE, t)
                free["misc", bank] = dve.mark(VE.tensor_copy(conv_sb[0:rowsn, i, :],
                                                             misc[0:rowsn, bank, 0:CW]))
            for c in range(KC):
                need(SP, (dve, dve.value))
                there = load(l_attn, wq_raw, w_q[c * P:(c + 1) * P, :])
                yield 5.0
                need(VE, there)
                for q in range(KQ):
                    i_ = wq_raw[:, q * P:(q + 1) * P].rearrange("p (h m a) -> p a m h", h=HH, a=2)
                    dve.mark(VE.tensor_copy(wq_sb[:, c, q, :, :, :], i_))
            need(SP, (dve, dve.value))
            load(l_attn, wmem_sb[:, :, :], w_mem.rearrange("(c p) n -> p c n", p=P))
            load(l_attn, wout_sb[:, :, :], w_out.rearrange("(v p) d -> p v d", p=P))
            yield 5.0

        together(attention_weights(), job0)
        section_joint()

        section(0, False, True)
        with nc.Fori(1, B - 1) as b:
            section(b, True, True)
        section(B - 1, True, False)
        for _ in ffn([(x2_dram, out, B - 1, load_weights)]):
            pass
        for ln in lines:
            need(SP, (ln, ln.value))


_INS = ["L0_attn_x", "L0_attn_W_mem", "L0_attn_conv_k", "L0_attn_W_q", "L0_attn_theta",
        "L0_attn_decay_slopes", "L0_attn_anchor_slopes", "L0_attn_score_scale", "L0_attn_W_re",
        "L0_attn_W_im", "L0_attn_norm_scale", "L0_attn_W_out", "L0_ffn_gate_w", "L0_ffn_w1",
        "L0_ffn_b1", "L0_ffn_w2", "L0_ffn_b2", "L0_ffn_shared_w1", "L0_ffn_shared_b1",
        "L0_ffn_shared_w2", "L0_ffn_shared_b2"]


def kernel(**inputs):
    import concourse.bacc as bacc
    from concourse.bass_utils import run_bass_kernel_spmd

    nc = bacc.Bacc("TRN2", target_bir_lowering=False, num_devices=1)
    arrays, args = {}, []
    for name in _INS:
        a = np.ascontiguousarray(inputs[name])
        arrays[f"in_{name}"] = a
        args.append(nc.dram_tensor(f"in_{name}", a.shape, mybir.dt.from_np(a.dtype),
                                   kind="ExternalInput").ap())
    args.append(nc.dram_tensor("out_rows", inputs["L0_attn_x"].shape, F32, kind="ExternalOutput").ap())
    macaron(nc, *args)
    r = run_bass_kernel_spmd(nc, [arrays], core_ids=[0])
    return r.results[0]["out_rows"]
```
